# Optimizing a Trainium2 kernel written in Bass

```python
import numpy as np
import jax
import jax.numpy as jnp

def _softmax(x, axis=-1):
    return jax.nn.softmax(x, axis=axis)

def _gelu(x):
    return jax.nn.gelu(x, approximate=True)

def _silu(x):
    return jax.nn.silu(x)

def _sigmoid(x):
    return jax.nn.sigmoid(x)

def _layernorm(x, axis=-1, eps=1e-05):
    m = jnp.mean(x, axis=axis, keepdims=True)
    v = jnp.var(x, axis=axis, keepdims=True)
    return (x - m) / jnp.sqrt(v + eps)

def _scatter_add(tgt, idx, src, axis=0):
    return tgt.at[idx].add(src)

def _segment_sum(src, seg, n):
    return jax.ops.segment_sum(src, seg, n)
kernel_name = 'mk_dlrm_tower_d1_rec_r8_59fab8'

def setup_inputs(seed: int=0):
    np.random.seed(seed)
    _w = jnp.asarray

    def _rec_inputs():
        import jax
        import jax.numpy as jnp
        _tk = jax.random.key(seed)
        dense_ctx = jax.random.normal(jax.random.fold_in(_tk, 190), (512, 16), jnp.float32)
        ids = jnp.stack([jax.random.randint(jax.random.fold_in(_tk, 200 + f), (512,), 0, v, jnp.int32) for f, v in enumerate([1250, 12500, 1250, 1250, 1000, 1000, 125000, 12500, 1250, 125000, 1250, 1000, 12500, 1000, 1000, 12500, 1000, 125000, 1250, 1000, 12500, 1250, 1000, 1250, 1000, 1250, 1000, 1250, 1000, 12500, 1250, 1000, 1250, 12500, 1250, 1250, 1000, 1000, 1000])], axis=1)
        tbl_0 = 0.05 * jax.random.normal(jax.random.fold_in(_tk, 500 + 0), (1250, 64), jnp.float32)
        tbl_1 = 0.05 * jax.random.normal(jax.random.fold_in(_tk, 500 + 1), (12500, 64), jnp.float32)
        tbl_2 = 0.05 * jax.random.normal(jax.random.fold_in(_tk, 500 + 2), (1250, 64), jnp.float32)
        tbl_3 = 0.05 * jax.random.normal(jax.random.fold_in(_tk, 500 + 3), (1250, 64), jnp.float32)
        tbl_4 = 0.05 * jax.random.normal(jax.random.fold_in(_tk, 500 + 4), (1000, 64), jnp.float32)
        tbl_5 = 0.05 * jax.random.normal(jax.random.fold_in(_tk, 500 + 5), (1000, 64), jnp.float32)
        tbl_6 = 0.05 * jax.random.normal(jax.random.fold_in(_tk, 500 + 6), (125000, 64), jnp.float32)
        tbl_7 = 0.05 * jax.random.normal(jax.random.fold_in(_tk, 500 + 7), (12500, 64), jnp.float32)
        tbl_8 = 0.05 * jax.random.normal(jax.random.fold_in(_tk, 500 + 8), (1250, 64), jnp.float32)
        tbl_9 = 0.05 * jax.random.normal(jax.random.fold_in(_tk, 500 + 9), (125000, 64), jnp.float32)
        tbl_10 = 0.05 * jax.random.normal(jax.random.fold_in(_tk, 500 + 10), (1250, 64), jnp.float32)
        tbl_11 = 0.05 * jax.random.normal(jax.random.fold_in(_tk, 500 + 11), (1000, 64), jnp.float32)
        tbl_12 = 0.05 * jax.random.normal(jax.random.fold_in(_tk, 500 + 12), (12500, 64), jnp.float32)
        tbl_13 = 0.05 * jax.random.normal(jax.random.fold_in(_tk, 500 + 13), (1000, 64), jnp.float32)
        tbl_14 = 0.05 * jax.random.normal(jax.random.fold_in(_tk, 500 + 14), (1000, 64), jnp.float32)
        tbl_15 = 0.05 * jax.random.normal(jax.random.fold_in(_tk, 500 + 15), (12500, 64), jnp.float32)
        tbl_16 = 0.05 * jax.random.normal(jax.random.fold_in(_tk, 500 + 16), (1000, 64), jnp.float32)
        tbl_17 = 0.05 * jax.random.normal(jax.random.fold_in(_tk, 500 + 17), (125000, 64), jnp.float32)
        tbl_18 = 0.05 * jax.random.normal(jax.random.fold_in(_tk, 500 + 18), (1250, 64), jnp.float32)
        tbl_19 = 0.05 * jax.random.normal(jax.random.fold_in(_tk, 500 + 19), (1000, 64), jnp.float32)
        tbl_20 = 0.05 * jax.random.normal(jax.random.fold_in(_tk, 500 + 20), (12500, 64), jnp.float32)
        tbl_21 = 0.05 * jax.random.normal(jax.random.fold_in(_tk, 500 + 21), (1250, 64), jnp.float32)
        tbl_22 = 0.05 * jax.random.normal(jax.random.fold_in(_tk, 500 + 22), (1000, 64), jnp.float32)
        tbl_23 = 0.05 * jax.random.normal(jax.random.fold_in(_tk, 500 + 23), (1250, 64), jnp.float32)
        tbl_24 = 0.05 * jax.random.normal(jax.random.fold_in(_tk, 500 + 24), (1000, 64), jnp.float32)
        tbl_25 = 0.05 * jax.random.normal(jax.random.fold_in(_tk, 500 + 25), (1250, 64), jnp.float32)
        tbl_26 = 0.05 * jax.random.normal(jax.random.fold_in(_tk, 500 + 26), (1000, 64), jnp.float32)
        tbl_27 = 0.05 * jax.random.normal(jax.random.fold_in(_tk, 500 + 27), (1250, 64), jnp.float32)
        tbl_28 = 0.05 * jax.random.normal(jax.random.fold_in(_tk, 500 + 28), (1000, 64), jnp.float32)
        tbl_29 = 0.05 * jax.random.normal(jax.random.fold_in(_tk, 500 + 29), (12500, 64), jnp.float32)
        tbl_30 = 0.05 * jax.random.normal(jax.random.fold_in(_tk, 500 + 30), (1250, 64), jnp.float32)
        tbl_31 = 0.05 * jax.random.normal(jax.random.fold_in(_tk, 500 + 31), (1000, 64), jnp.float32)
        tbl_32 = 0.05 * jax.random.normal(jax.random.fold_in(_tk, 500 + 32), (1250, 64), jnp.float32)
        tbl_33 = 0.05 * jax.random.normal(jax.random.fold_in(_tk, 500 + 33), (12500, 64), jnp.float32)
        tbl_34 = 0.05 * jax.random.normal(jax.random.fold_in(_tk, 500 + 34), (1250, 64), jnp.float32)
        tbl_35 = 0.05 * jax.random.normal(jax.random.fold_in(_tk, 500 + 35), (1250, 64), jnp.float32)
        tbl_36 = 0.05 * jax.random.normal(jax.random.fold_in(_tk, 500 + 36), (1000, 64), jnp.float32)
        tbl_37 = 0.05 * jax.random.normal(jax.random.fold_in(_tk, 500 + 37), (1000, 64), jnp.float32)
        tbl_38 = 0.05 * jax.random.normal(jax.random.fold_in(_tk, 500 + 38), (1000, 64), jnp.float32)
        _rk = jax.random.fold_in(_tk, 7)
        W_top1 = 0.0363456 * jax.random.normal(jax.random.fold_in(_tk, 801), (757, 512), jnp.float32)
        W_top2 = 0.0441942 * jax.random.normal(jax.random.fold_in(_tk, 802), (512, 256), jnp.float32)
        W_top3 = 0.0625 * jax.random.normal(jax.random.fold_in(_tk, 803), (256, 1), jnp.float32)
        b_top1 = jnp.zeros((512,), jnp.float32)
        b_top2 = jnp.zeros((256,), jnp.float32)
        return (dense_ctx, ids, tbl_0, tbl_1, tbl_2, tbl_3, tbl_4, tbl_5, tbl_6, tbl_7, tbl_8, tbl_9, tbl_10, tbl_11, tbl_12, tbl_13, tbl_14, tbl_15, tbl_16, tbl_17, tbl_18, tbl_19, tbl_20, tbl_21, tbl_22, tbl_23, tbl_24, tbl_25, tbl_26, tbl_27, tbl_28, tbl_29, tbl_30, tbl_31, tbl_32, tbl_33, tbl_34, tbl_35, tbl_36, tbl_37, tbl_38, W_top1, b_top1, W_top2, b_top2, W_top3)
    dense_ctx, ids, tbl_0, tbl_1, tbl_2, tbl_3, tbl_4, tbl_5, tbl_6, tbl_7, tbl_8, tbl_9, tbl_10, tbl_11, tbl_12, tbl_13, tbl_14, tbl_15, tbl_16, tbl_17, tbl_18, tbl_19, tbl_20, tbl_21, tbl_22, tbl_23, tbl_24, tbl_25, tbl_26, tbl_27, tbl_28, tbl_29, tbl_30, tbl_31, tbl_32, tbl_33, tbl_34, tbl_35, tbl_36, tbl_37, tbl_38, W_top1, b_top1, W_top2, b_top2, W_top3 = _rec_inputs()

    def _L0_rec_setup():
        import jax, jax.numpy as jnp
        import numpy as np
        NUM_FIELDS = 39
        _ROW, _COL = np.triu_indices(NUM_FIELDS, k=1)
        key = jax.random.key(seed)
        x = jax.random.normal(key, (2048, NUM_FIELDS, 64), dtype=jnp.float32)
        return {'x': x}
    _L0_rec_all = _L0_rec_setup()
    _L0_rec_in = {k: v for k, v in _L0_rec_all.items() if k in ()}
    del _L0_rec_all
    return {'dense_ctx': dense_ctx, 'ids': ids, 'tbl_0': tbl_0, 'tbl_1': tbl_1, 'tbl_2': tbl_2, 'tbl_3': tbl_3, 'tbl_4': tbl_4, 'tbl_5': tbl_5, 'tbl_6': tbl_6, 'tbl_7': tbl_7, 'tbl_8': tbl_8, 'tbl_9': tbl_9, 'tbl_10': tbl_10, 'tbl_11': tbl_11, 'tbl_12': tbl_12, 'tbl_13': tbl_13, 'tbl_14': tbl_14, 'tbl_15': tbl_15, 'tbl_16': tbl_16, 'tbl_17': tbl_17, 'tbl_18': tbl_18, 'tbl_19': tbl_19, 'tbl_20': tbl_20, 'tbl_21': tbl_21, 'tbl_22': tbl_22, 'tbl_23': tbl_23, 'tbl_24': tbl_24, 'tbl_25': tbl_25, 'tbl_26': tbl_26, 'tbl_27': tbl_27, 'tbl_28': tbl_28, 'tbl_29': tbl_29, 'tbl_30': tbl_30, 'tbl_31': tbl_31, 'tbl_32': tbl_32, 'tbl_33': tbl_33, 'tbl_34': tbl_34, 'tbl_35': tbl_35, 'tbl_36': tbl_36, 'tbl_37': tbl_37, 'tbl_38': tbl_38, 'W_top1': W_top1, 'b_top1': b_top1, 'W_top2': W_top2, 'b_top2': b_top2, 'W_top3': W_top3}

def reference(dense_ctx, ids, tbl_0, tbl_1, tbl_2, tbl_3, tbl_4, tbl_5, tbl_6, tbl_7, tbl_8, tbl_9, tbl_10, tbl_11, tbl_12, tbl_13, tbl_14, tbl_15, tbl_16, tbl_17, tbl_18, tbl_19, tbl_20, tbl_21, tbl_22, tbl_23, tbl_24, tbl_25, tbl_26, tbl_27, tbl_28, tbl_29, tbl_30, tbl_31, tbl_32, tbl_33, tbl_34, tbl_35, tbl_36, tbl_37, tbl_38, W_top1, b_top1, W_top2, b_top2, W_top3):
    import jax
    import jax.numpy as jnp

    def _L0_rec_ref(x):
        import jax, jax.numpy as jnp
        import numpy as np
        NUM_FIELDS = 39
        _ROW, _COL = np.triu_indices(NUM_FIELDS, k=1)
        s = jnp.sum(x, axis=-1)
        return s[:, _ROW] * s[:, _COL]
    e = jnp.stack([tbl_0[ids[:, 0]], tbl_1[ids[:, 1]], tbl_2[ids[:, 2]], tbl_3[ids[:, 3]], tbl_4[ids[:, 4]], tbl_5[ids[:, 5]], tbl_6[ids[:, 6]], tbl_7[ids[:, 7]], tbl_8[ids[:, 8]], tbl_9[ids[:, 9]], tbl_10[ids[:, 10]], tbl_11[ids[:, 11]], tbl_12[ids[:, 12]], tbl_13[ids[:, 13]], tbl_14[ids[:, 14]], tbl_15[ids[:, 15]], tbl_16[ids[:, 16]], tbl_17[ids[:, 17]], tbl_18[ids[:, 18]], tbl_19[ids[:, 19]], tbl_20[ids[:, 20]], tbl_21[ids[:, 21]], tbl_22[ids[:, 22]], tbl_23[ids[:, 23]], tbl_24[ids[:, 24]], tbl_25[ids[:, 25]], tbl_26[ids[:, 26]], tbl_27[ids[:, 27]], tbl_28[ids[:, 28]], tbl_29[ids[:, 29]], tbl_30[ids[:, 30]], tbl_31[ids[:, 31]], tbl_32[ids[:, 32]], tbl_33[ids[:, 33]], tbl_34[ids[:, 34]], tbl_35[ids[:, 35]], tbl_36[ids[:, 36]], tbl_37[ids[:, 37]], tbl_38[ids[:, 38]]], axis=1)
    z = _L0_rec_ref(e)
    z = z.reshape(z.shape[0], -1)
    h = jnp.concatenate([z, dense_ctx], axis=1)
    h = jnp.maximum(h @ W_top1 + b_top1, 0.0)
    h = jnp.maximum(h @ W_top2 + b_top2, 0.0)
    y = h @ W_top3
    return y

_drawn_inputs = setup_inputs


def setup_inputs(seed=0):
    import zlib

    import numpy as np

    out = dict(_drawn_inputs(seed))
    spreads = {'b_top1': (0.0, 0.1), 'b_top2': (0.0, 0.1)}
    factors = {}
    for name, (base, spread) in spreads.items():
        noise = np.random.default_rng([zlib.crc32(name.encode()), seed]).standard_normal(out[name].shape)
        drawn = base * np.exp(spread * noise) if base else spread * noise
        out[name] = jnp.asarray(drawn.astype(out[name].dtype))
    for name, factor in factors.items():
        out[name] = (out[name] * factor).astype(out[name].dtype)
    return out
```

```python
from contextlib import ExitStack

import numpy as np

import concourse.bass as bass
from concourse import mybir

P = 128
BATCH, NUM_FIELDS, DIM, DENSE = 512, 39, 64, 16
HIDDEN1, HIDDEN2 = 512, 256
TILES = BATCH // P
SPLIT = 3
SET = 32

BLOCKS = {0: 10, 1: 98, 2: 10, 3: 10, 4: 8, 5: 8, 6: 977, 7: 98, 8: 10, 9: 977, 10: 10, 11: 8, 12: 98,
          13: 8, 14: 8, 15: 98, 16: 8, 17: 977, 18: 10, 19: 8, 20: 98, 21: 10, 22: 8, 23: 10, 24: 8,
          25: 10, 26: 8, 27: 10, 28: 8, 29: 98, 30: 10, 31: 8, 32: 10, 33: 98, 34: 10, 35: 10, 36: 8,
          37: 8, 38: 8}
WIDE, NARROW = 10, 8
SMALL = [f for f in range(NUM_FIELDS) if BLOCKS[f] == WIDE] + [f for f in range(NUM_FIELDS) if BLOCKS[f] == NARROW]
LARGE = [f for f in range(NUM_FIELDS) if BLOCKS[f] > WIDE]
NS, NL = len(SMALL), len(LARGE)

GROUPS = [(0, 4, WIDE), (4, 4, WIDE), (8, 2, WIDE), (10, 4, WIDE), (14, 5, NARROW), (19, 5, NARROW), (24, 5, NARROW)]
FIRST_BLOCK = [sum(n * b for _, n, b in GROUPS[:g]) for g in range(len(GROUPS) + 1)]
ALL_BLOCKS = FIRST_BLOCK[-1]
SET_START = [0, 10, 19, NS]
PLACE = {}
for _i, _f in enumerate(SMALL):
    _s = max(s for s in range(3) if SET_START[s] <= _i)
    PLACE[_f] = SET * _s + SPLIT * (_i - SET_START[_s])
for _i, _f in enumerate(LARGE):
    PLACE[_f] = SET * 3 + SPLIT * _i

KEPT = 102
CHUNK_PAIRS = [128, 128, 128, 127, 128, KEPT]
CHUNK_ROWS = CHUNK_PAIRS[:-1] + [KEPT + DENSE + 1]
CHUNKS = len(CHUNK_PAIRS)


def chunks_of_pairs():
    small = {f: n for n, f in enumerate(SMALL)}
    ready = {0: [], 1: [], 2: [], 3: [], 4: []}
    for i in range(NUM_FIELDS):
        for j in range(i + 1, NUM_FIELDS):
            last = max(small.get(i, -1), small.get(j, -1))
            is_large = i not in small or j not in small
            if is_large:
                ready[3 if last < SET_START[2] else 4].append((i, j))
            else:
                ready[0 if last < SET_START[2] else 1 if last < GROUPS[6][0] else 2].append((i, j))
    first, rest = ready[0][:128], ready[0][128:]
    middle = ready[3] + rest[:256 - len(ready[3])]
    rest = rest[256 - len(ready[3]):] + ready[1]
    chunks = [first, middle[:128], middle[128:], rest, ready[2][:128], ready[2][128:] + ready[4]]
    assert [len(c) for c in chunks] == CHUNK_PAIRS and sum(CHUNK_PAIRS) == NUM_FIELDS * (NUM_FIELDS - 1) // 2
    return chunks


STEPS = [((0,), 0, 4), ((1, 2), 0, 2), ((3,), 0, 4), ((4,), 0, 4), ((1, 2), 2, 3), ((5,), 0, 3), ((1, 2, 5), 3, 4)]
EARLY = 3
TURNS = [(0, 64, 0, 4), (96, 128, 0, 2), (64, 96, 0, 4), (64, 96, 0, 4), (96, 128, 2, 3), (96, 128, 3, 4)]


def build(nc, ids, tables, large, consts, selectors, quad_w, w1, w2, dense_t, out):
    fp32, bf16, i32 = mybir.dt.float32, mybir.dt.bfloat16, mybir.dt.int32
    ALU, ACT, AX = mybir.AluOpType, mybir.ActivationFunctionType, mybir.AxisListType

    with ExitStack() as ctx:
        def sb(name, shape, dt):
            return ctx.enter_context(nc.sbuf_tensor(name, shape, dt))

        def sem(name):
            return ctx.enter_context(nc.semaphore(name))

        n_ids = TILES * NS
        ids_sb = sb("ids_sb", [P, TILES * NL + 2 * n_ids], i32)
        gather_ids = ids_sb[:, 0:TILES * NL]
        block_ids = ids_sb[:, TILES * NL:TILES * NL + n_ids]
        flat_ids = ids_sb[:, TILES * NL + n_ids:]
        block_of = sb("block_of", [P, n_ids], i32)
        row_of = sb("row_of", [P, n_ids], i32)
        row_sq = sb("row_sq", [P, n_ids], i32)
        row_sq_digit = sb("row_sq_digit", [P, 2, n_ids], i32)
        digits = sb("digits", [P, 3, n_ids], bf16)
        query = sb("query", [3, NS * BATCH], bf16)
        quad_w_sb = sb("quad_w_sb", [3, P], bf16)
        consts_sb = sb("consts_sb", [P, 1 + WIDE + 4], fp32)
        one_minus_sq = consts_sb[:, 0:1]
        block_iota = consts_sb[:, 1:1 + WIDE]
        b2_sb = consts_sb[:, 1 + WIDE:3 + WIDE]
        w3_sb = consts_sb[:, 3 + WIDE:5 + WIDE]
        sel_sb = sb("sel_sb", [P, 2 * CHUNKS + 1, P], bf16)
        ident = sel_sb[:, 2 * CHUNKS, :]
        tables_sb = sb("tables_sb", [P, ALL_BLOCKS, DIM], fp32)
        gathered = sb("gathered", [P, TILES, NL, DIM], fp32)
        row_sums = sb("row_sums", [P, ALL_BLOCKS], fp32)
        row_rest = sb("row_rest", [P, ALL_BLOCKS], fp32)
        row_parts = sb("row_parts", [P, SPLIT * ALL_BLOCKS], bf16)
        large_sums = sb("large_sums", [P, TILES, NL], fp32)
        large_rest = sb("large_rest", [P, TILES, NL], fp32)
        onehot = sb("onehot", [P, NS, BATCH], bf16)
        mask = sb("mask", [P, TILES * ALL_BLOCKS], bf16)
        masked = sb("masked", [P, 2, 512], fp32)
        parts = sb("parts", [P, TILES, P], bf16)
        parts_t = sb("parts_t", [P, BATCH], bf16)
        left = sb("left", [P, 2, 512], fp32)
        z = sb("z", [P, CHUNKS, BATCH], fp32)
        w1_sb = sb("w1_sb", [P, CHUNKS, HIDDEN1], fp32)
        w2_sb = sb("w2_sb", [P, HIDDEN1 // P, HIDDEN2], fp32)
        h1 = sb("h1", [P, HIDDEN1 // P, BATCH], fp32)
        h2 = sb("h2", [P, HIDDEN2 // P, BATCH], fp32)
        y = sb("y", [1, BATCH], fp32)

        h1_ps = ctx.enter_context(nc.psum_tensor("h1_ps", [P, HIDDEN1 // P, 512], fp32))
        pair_ps = ctx.enter_context(nc.psum_tensor("pair_ps", [P, 2, 512], fp32))
        look_ps = ctx.enter_context(nc.psum_tensor("look_ps", [P, 512], fp32))
        turn_ps = ctx.enter_context(nc.psum_tensor("turn_ps", [P, 512], fp32))
        turn_bf = [ps.bitcast(bf16) for ps in [turn_ps[:, :]] * (len(TURNS) - 1) + [pair_ps[:, 0, :]]]
        h2_ps = [look_ps, turn_ps]
        y_ps = pair_ps[0:1, 1, :]

        ids_loaded = sem("ids_loaded")
        consts_loaded = sem("consts_loaded")
        quad_w_loaded = sem("quad_w_loaded")
        sel_loaded = sem("sel_loaded")
        tables_loaded = [sem(f"tables_loaded_{g}") for g in range(len(GROUPS))]
        w1_loaded = [sem(f"w1_loaded_{n}") for n in range(2)]
        w2_loaded = sem("w2_loaded")
        dense_loaded = sem("dense_loaded")
        query_loaded = sem("query_loaded")
        rows_gathered = [sem(f"rows_gathered_{t}") for t in range(TILES)]
        out_stored = sem("out_stored")
        zeros_set = sem("zeros_set")
        dve_steps = sem("dve_steps")
        digits_ready = sem("digits_ready")
        quads_ready = sem("quads_ready")
        onehots_ready = sem("onehots_ready")
        row_parts_ready = sem("row_parts_ready")
        lookups_ready = sem("lookups_ready")
        lookups_masked = sem("lookups_masked")
        small_parts_ready = sem("small_parts_ready")
        large_parts_ready = sem("large_parts_ready")
        turned = sem("turned")
        parts_t_ready = sem("parts_t_ready")
        pairs_selected = sem("pairs_selected")
        left_copied = sem("left_copied")
        z_ready = sem("z_ready")
        layer1_done = sem("layer1_done")
        h1_ready_act = sem("h1_ready_act")
        h1_ready_dve = sem("h1_ready_dve")
        layer2_done = sem("layer2_done")
        h2_ready_act = sem("h2_ready_act")
        h2_ready_dve = sem("h2_ready_dve")
        layer3_done = sem("layer3_done")
        y_ready = sem("y_ready")

        block = ctx.enter_context(nc.Block())

        @block.sync
        def _(sp):
            sp.dma_start(ids_sb[:, :], ids).then_inc(ids_loaded, 16)

            def load_tables(g):
                part = slice(FIRST_BLOCK[g], FIRST_BLOCK[g + 1])
                sp.dma_start(tables_sb[:, part, :], tables[:, part, :]).then_inc(tables_loaded[g], 16)

            load_tables(0)
            sp.wait_ge(digits_ready, 1)
            for k in range(3):
                sp.dma_start(query[k:k + 1, :].rearrange("k (p n) -> k p n", p=P), digits[:, k, :])\
                  .then_inc(query_loaded, 16)
            for g in range(1, 4):
                load_tables(g)
            sp.dma_start(sel_sb[:, :, :], selectors).then_inc(sel_loaded, 16)
            load_tables(4)
            sp.dma_start(w1_sb[:, 0:3, :], w1[:, 0:3, :]).then_inc(w1_loaded[0], 16)
            load_tables(5)
            load_tables(6)
            sp.dma_start(z[KEPT:CHUNK_ROWS[-1], CHUNKS - 1, :], dense_t).then_inc(dense_loaded, 16)
            sp.dma_start(w1_sb[:, 3:CHUNKS, :], w1[:, 3:CHUNKS, :]).then_inc(w1_loaded[1], 16)
            sp.dma_start(w2_sb[:, :, :], w2).then_inc(w2_loaded, 16)
            sp.wait_ge(y_ready, 1)
            sp.dma_start(out.rearrange("b a -> a b"), y[:, :]).then_inc(out_stored, 16)
            sp.wait_ge(out_stored, 16)

        @block.gpsimd
        def _(pool):
            pool.memset(parts[:, :, :], 0.0).then_inc(zeros_set, 1)
            pool.memset(parts_t[:, :], 0.0).then_inc(zeros_set, 1)
            pool.wait_ge(ids_loaded, 16)
            for t in range(TILES):
                for n in range(NL):
                    k = t * NL + n
                    pool.indirect_dma_start(
                        out=gathered[:, t, n, :], out_offset=None, in_=large[n],
                        in_offset=bass.IndirectOffsetOnAxis(ap=gather_ids[:, k:k + 1], axis=0))\
                        .then_inc(rows_gathered[t], 16)

        @block.scalar
        def _(act):
            act.dma_start(consts_sb[:, :], consts).then_inc(consts_loaded, 16)
            act.dma_start(quad_w_sb[:, :], quad_w).then_inc(quad_w_loaded, 16)
            act.wait_ge(consts_loaded, 16)
            for f in range(NS):
                act.wait_ge(quads_ready, f + 1)
                nc.scalar.activation(onehot[:, f, :], pair_ps[:, f % 2, :], ACT.Relu, bias=one_minus_sq)\
                  .then_inc(onehots_ready, 1)

            def copy_turn(n):
                c0, c1, t0, t1 = TURNS[n]
                act.wait_ge(turned, n + 1)
                if n == 0:
                    act.wait_ge(zeros_set, 2)
                nc.scalar.activation(parts_t[c0:c1, t0 * P:t1 * P], turn_bf[n][c0:c1, t0 * P:t1 * P],
                                     ACT.Copy)\
                  .then_inc(parts_t_ready, 1)

            def copy_left(n):
                chunks, t0, t1 = STEPS[n]
                width = len(chunks) * (t1 - t0) * P
                act.wait_ge(pairs_selected, n + 1)
                if n >= 2:
                    act.wait_ge(z_ready, n - 1)
                nc.scalar.activation(left[:, n % 2, 0:width], pair_ps[:, 0, 0:width], ACT.Copy)\
                  .then_inc(left_copied, 1)

            def relu1(n, t0, t1):
                act.wait_ge(layer1_done, n + 1)
                nc.scalar.activation(h1[:, 0:2, t0 * P:t1 * P], h1_ps[:, 0:2, t0 * P:t1 * P], ACT.Relu)\
                  .then_inc(h1_ready_act, 1)

            def relu2(n, t0, t1):
                act.wait_ge(layer2_done, 2 * n + 1)
                nc.scalar.activation(h2[:, 0, t0 * P:t1 * P], h2_ps[0][:, t0 * P:t1 * P], ACT.Relu,
                                     bias=b2_sb[:, 0:1]).then_inc(h2_ready_act, 1)

            copy_turn(0)
            copy_turn(1)
            copy_left(0)
            copy_left(1)
            copy_turn(2)
            copy_left(2)
            copy_turn(3)
            copy_turn(4)
            copy_left(3)
            copy_left(4)
            copy_left(5)
            relu1(0, 0, EARLY)
            copy_turn(5)
            copy_left(6)
            relu2(0, 0, EARLY)
            relu1(1, EARLY, TILES)
            relu2(1, EARLY, TILES)

        @block.tensor
        def _(pe):
            def quads(g):
                first, count, _ = GROUPS[g]
                for f in range(first, first + count):
                    if f >= 2:
                        pe.wait_ge(onehots_ready, f - 1)
                    nc.tensor.matmul(pair_ps[:, f % 2, :], quad_w_sb[:, :], query[:, f * BATCH:(f + 1) * BATCH],
                                     start=True, stop=True).then_inc(quads_ready, 1)

            def lookups(g):
                first, count, blocks = GROUPS[g]
                n = SPLIT * blocks
                pe.wait_ge(row_parts_ready, g + 1)
                pe.wait_ge(onehots_ready, first + count)
                if g >= 1:
                    pe.wait_ge(lookups_masked, g)
                for t in range(TILES):
                    for f in range(count):
                        at = (t * count + f) * n
                        src = SPLIT * FIRST_BLOCK[g] + f * n
                        last = nc.tensor.matmul(look_ps[:, at:at + n], onehot[:, first + f, t * P:(t + 1) * P],
                                                row_parts[:, src:src + n], start=True, stop=True)
                last.then_inc(lookups_ready, 1)

            def turn(n):
                c0, c1, t0, t1 = TURNS[n]
                for t in range(t0, t1):
                    last = nc.tensor.transpose(turn_bf[n][c0:c1, t * P:(t + 1) * P], parts[:, t, c0:c1], ident)
                last.then_inc(turned, 1)

            def select(n):
                chunks, t0, t1 = STEPS[n]
                w = (t1 - t0) * P
                rows = {0: 64, 2: 96, 3: 96}.get(n, P)
                if n >= 1:
                    pe.wait_ge(z_ready, n)
                for side in range(2):
                    for i, c in enumerate(chunks):
                        last = nc.tensor.matmul(pair_ps[:, side, i * w:(i + 1) * w], sel_sb[0:rows, 2 * c + side, :],
                                                parts_t[0:rows, t0 * P:t1 * P], start=True, stop=True)
                last.then_inc(pairs_selected, 1)

            def layer1(n):
                chunks, t0, t1 = STEPS[n]
                pe.wait_ge(z_ready, n + 1)
                for c in chunks:
                    rows = CHUNK_ROWS[c]
                    for m in range(HIDDEN1 // P):
                        last = nc.tensor.matmul(h1_ps[:, m, t0 * P:t1 * P], w1_sb[0:rows, c, m * P:(m + 1) * P],
                                                z[0:rows, c, t0 * P:t1 * P], start=(n == 0), stop=(c == CHUNKS - 1),
                                                skip_group_check=True)
                if CHUNKS - 1 in chunks:
                    last.then_inc(layer1_done, 1)

            def layer2(n, t0, t1):
                pe.wait_ge(h1_ready_act, n + 1)
                for m in range(HIDDEN2 // P):
                    for k in range(HIDDEN1 // P):
                        if m == 0 and k == 2:
                            pe.wait_ge(h1_ready_dve, n + 1)
                        last = nc.tensor.matmul(h2_ps[m][:, t0 * P:t1 * P], w2_sb[:, k, m * P:(m + 1) * P],
                                                h1[:, k, t0 * P:t1 * P], start=(k == 0), stop=(k == HIDDEN1 // P - 1))
                    last.then_inc(layer2_done, 1)

            def layer3(n, t0, t1):
                for k in range(HIDDEN2 // P):
                    pe.wait_ge(h2_ready_act if k == 0 else h2_ready_dve, n + 1)
                    last = nc.tensor.matmul(y_ps[:, t0 * P:t1 * P], w3_sb[:, k:k + 1],
                                            h2[:, k, t0 * P:t1 * P], start=(k == 0), stop=(k == HIDDEN2 // P - 1))
                last.then_inc(layer3_done, 1)

            pe.wait_ge(quad_w_loaded, 16)
            pe.wait_ge(query_loaded, 3 * 16)
            quads(0)
            for g in range(4):
                quads(g + 1)
                lookups(g)
            quads(5)
            quads(6)
            lookups(4)
            pe.wait_ge(sel_loaded, 16)
            pe.wait_ge(small_parts_ready, 5)
            turn(0)
            pe.wait_ge(large_parts_ready, 2)
            turn(1)
            pe.wait_ge(onehots_ready, NS)
            pe.wait_ge(parts_t_ready, 1)
            select(0)
            lookups(5)
            pe.wait_ge(parts_t_ready, 2)
            select(1)
            pe.wait_ge(w1_loaded[0], 16)
            layer1(0)
            pe.wait_ge(small_parts_ready, 6)
            turn(2)
            layer1(1)
            lookups(6)
            pe.wait_ge(parts_t_ready, 3)
            select(2)
            pe.wait_ge(small_parts_ready, 7)
            turn(3)
            pe.wait_ge(large_parts_ready, 3)
            turn(4)
            pe.wait_ge(w1_loaded[1], 16)
            layer1(2)
            pe.wait_ge(parts_t_ready, 4)
            select(3)
            pe.wait_ge(parts_t_ready, 5)
            select(4)
            layer1(3)
            select(5)
            layer1(4)
            pe.wait_ge(dense_loaded, 16)
            layer1(5)
            pe.wait_ge(w2_loaded, 16)
            layer2(0, 0, EARLY)
            pe.wait_ge(large_parts_ready, 4)
            turn(5)
            pe.wait_ge(parts_t_ready, 6)
            select(6)
            layer1(6)
            layer3(0, 0, EARLY)
            layer2(1, EARLY, TILES)
            layer3(1, EARLY, TILES)

        @block.vector
        def _(dve):
            chain = [0]

            def link(instruction):
                chain[0] += 1
                instruction.then_inc(dve_steps, 1)
                dve.wait_ge(dve_steps, chain[0])

            def split(total, rest, hi, mid, lo, done):
                link(nc.vector.tensor_copy(hi, total))
                link(nc.vector.tensor_tensor(rest, total, hi, ALU.subtract))
                link(nc.vector.tensor_copy(mid, rest))
                nc.vector.tensor_tensor(lo, rest, mid, ALU.subtract).then_inc(done, 1)

            def sum_rows(g):
                part = slice(FIRST_BLOCK[g], FIRST_BLOCK[g + 1])
                dve.wait_ge(tables_loaded[g], 16)
                link(nc.vector.tensor_reduce(row_sums[:, part], tables_sb[:, part, :], op=ALU.add, axis=AX.X))

            def split_rows(g):
                _, count, blocks = GROUPS[g]
                a, b = FIRST_BLOCK[g], FIRST_BLOCK[g + 1]
                by_part = row_parts[:, SPLIT * a:SPLIT * b].rearrange("p (f s c) -> p f s c", s=SPLIT, c=blocks)
                split(row_sums[:, a:b].rearrange("p (f c) -> p f c", c=blocks),
                      row_rest[:, a:b].rearrange("p (f c) -> p f c", c=blocks),
                      by_part[:, :, 0, :], by_part[:, :, 1, :], by_part[:, :, 2, :], row_parts_ready)

            def mask_lookups(g):
                first, count, blocks = GROUPS[g]
                n = TILES * count
                a = FIRST_BLOCK[g]
                keep = mask[:, TILES * a:TILES * FIRST_BLOCK[g + 1]].rearrange("p (n c) -> p n c", c=blocks)
                keep = keep.unsqueeze(2).to_broadcast([P, n, SPLIT, blocks])
                dve.wait_ge(lookups_ready, g + 1)
                kept = masked[:, g % 2, 0:n * SPLIT * blocks]
                nc.vector.tensor_tensor(
                    kept.rearrange("p (n s c) -> p n s c", s=SPLIT, c=blocks),
                    look_ps[:, 0:n * SPLIT * blocks].rearrange("p (n s c) -> p n s c", s=SPLIT, c=blocks),
                    keep, ALU.mult).then_inc(lookups_masked, 1)
                dve.wait_ge(lookups_masked, g + 1)
                place = PLACE[SMALL[first]]
                with nc.allow_low_precision(reason="a sum of one bfloat16 value and zeros is exact"):
                    nc.vector.tensor_reduce(parts[:, :, place:place + SPLIT * count],
                                            kept.rearrange("p (t m c) -> p t m c", t=TILES, c=blocks),
                                            op=ALU.add, axis=AX.X).then_inc(small_parts_ready, 1)

            def large_parts(t):
                dve.wait_ge(rows_gathered[t], NL * 16)
                link(nc.vector.tensor_reduce(large_sums[:, t, :], gathered[:, t, :, :], op=ALU.add, axis=AX.X))
                by_part = parts[:, t, 3 * SET:3 * SET + SPLIT * NL].rearrange("p (f s) -> p f s", s=SPLIT)
                split(large_sums[:, t, :], large_rest[:, t, :], by_part[:, :, 0], by_part[:, :, 1], by_part[:, :, 2],
                      large_parts_ready)

            def multiply_pairs(n):
                chunks, t0, t1 = STEPS[n]
                w = (t1 - t0) * P
                full = [c for c in chunks if c < CHUNKS - 1]
                dve.wait_ge(left_copied, n + 1)
                pieces = [(0, full, P)] if full else []
                if CHUNKS - 1 in chunks:
                    pieces.append((len(full), [CHUNKS - 1], KEPT))
                for i, cs, rows in pieces:
                    cols = slice(i * w, (i + len(cs)) * w)
                    last = nc.vector.tensor_tensor(
                        z[0:rows, cs[0]:cs[0] + len(cs), t0 * P:t1 * P],
                        pair_ps[0:rows, 1, cols].rearrange("p (c w) -> p c w", w=w),
                        left[0:rows, n % 2, cols].rearrange("p (c w) -> p c w", w=w), ALU.mult)
                last.then_inc(z_ready, 1)

            def relu1(n, t0, t1):
                dve.wait_ge(layer1_done, n + 1)
                nc.vector.tensor_scalar(h1[:, 2:4, t0 * P:t1 * P], h1_ps[:, 2:4, t0 * P:t1 * P], 0.0, None, ALU.max)\
                  .then_inc(h1_ready_dve, 1)

            def relu2(n, t0, t1):
                dve.wait_ge(layer2_done, 2 * n + 2)
                nc.vector.tensor_scalar(h2[:, 1, t0 * P:t1 * P], h2_ps[1][:, t0 * P:t1 * P], b2_sb[:, 1:2], 0.0,
                                        ALU.add, ALU.max).then_inc(h2_ready_dve, 1)

            dve.wait_ge(ids_loaded, 16)
            link(nc.vector.tensor_scalar(row_of[:, :], flat_ids, P - 1, None, ALU.bitwise_and))
            nc.vector.tensor_copy(digits[:, 2, :], row_of[:, :])
            link(nc.vector.tensor_tensor(row_sq[:, :], row_of[:, :], row_of[:, :], ALU.mult))
            nc.vector.tensor_scalar(row_sq_digit[:, 0, :], row_sq[:, :], 7, None, ALU.logical_shift_right)
            link(nc.vector.tensor_scalar(row_sq_digit[:, 1, :], row_sq[:, :], P - 1, None, ALU.bitwise_and))
            nc.vector.tensor_copy(digits[:, 0:2, :], row_sq_digit[:, :, :]).then_inc(digits_ready, 1)
            link(nc.vector.tensor_scalar(block_of[:, :], block_ids, 7, None, ALU.logical_shift_right))
            dve.wait_ge(consts_loaded, 16)
            n_wide = GROUPS[3][0] + GROUPS[3][1]
            for a, b, blocks in ((0, n_wide, WIDE), (n_wide, NS, NARROW)):
                n = TILES * (b - a)
                at = TILES * WIDE * a
                link(nc.vector.tensor_tensor(
                    mask[:, at:at + n * blocks].rearrange("p (n c) -> p n c", c=blocks),
                    block_of[:, TILES * a:TILES * b].unsqueeze(2).to_broadcast([P, n, blocks]),
                    block_iota[:, 0:blocks].unsqueeze(1).to_broadcast([P, n, blocks]), ALU.is_equal))
            dve.wait_ge(zeros_set, 2)
            for g in range(5):
                sum_rows(g)
                split_rows(g)
                if g >= 1:
                    mask_lookups(g - 1)
                if g == 3:
                    large_parts(0)
            sum_rows(5)
            mask_lookups(4)
            large_parts(1)
            split_rows(5)
            multiply_pairs(0)
            sum_rows(6)
            multiply_pairs(1)
            split_rows(6)
            mask_lookups(5)
            mask_lookups(6)
            multiply_pairs(2)
            large_parts(2)
            for n in (3, 4, 5):
                multiply_pairs(n)
            relu1(0, 0, EARLY)
            large_parts(3)
            multiply_pairs(6)
            relu2(0, 0, EARLY)
            relu1(1, EARLY, TILES)
            relu2(1, EARLY, TILES)
            dve.wait_ge(layer3_done, 2)
            nc.vector.tensor_copy(y[:, :], y_ps).then_inc(y_ready, 1)


def kernel(**inputs):
    import ml_dtypes
    import concourse.bacc as bacc
    from concourse.bass_utils import run_bass_kernel_spmd

    a = {k: np.asarray(v) for k, v in inputs.items()}
    for f in range(NUM_FIELDS):
        assert -(-a[f"tbl_{f}"].shape[0] // P) == BLOCKS[f]

    ids = a["ids"]
    by_tile = ids.reshape(TILES, P, NUM_FIELDS).transpose(1, 0, 2)
    ids_all = np.concatenate(
        [by_tile[:, :, LARGE].reshape(P, -1)]
        + [by_tile[:, :, SMALL[s:s + n]].reshape(P, -1) for s, n, _ in GROUPS]
        + [np.ascontiguousarray(ids[:, SMALL].T).reshape(P, -1)], axis=1)

    def blocked(f):
        rows = a[f"tbl_{f}"]
        padded = np.zeros((BLOCKS[f] * P, DIM), rows.dtype)
        padded[:rows.shape[0]] = rows
        return padded.reshape(BLOCKS[f], P, DIM).transpose(1, 0, 2)

    tables = np.concatenate([blocked(f) for f in SMALL], axis=1)

    chunks = chunks_of_pairs()
    number = {}
    for i in range(NUM_FIELDS):
        for j in range(i + 1, NUM_FIELDS):
            number[i, j] = len(number)
    w1 = np.zeros((P, CHUNKS, HIDDEN1), np.float32)
    selectors = np.zeros((P, 2 * CHUNKS + 1, P), ml_dtypes.bfloat16)
    for c, pairs in enumerate(chunks):
        w1[:len(pairs), c] = a["W_top1"][[number[p] for p in pairs]]
        for r, pair in enumerate(pairs):
            for side in range(2):
                selectors[PLACE[pair[side]]:PLACE[pair[side]] + SPLIT, 2 * c + side, r] = 1
    selectors[:, 2 * CHUNKS] = np.eye(P)
    w1[KEPT:KEPT + DENSE, CHUNKS - 1] = a["W_top1"][len(number):]
    w1[KEPT + DENSE, CHUNKS - 1] = a["b_top1"]
    dense_t = np.concatenate([a["dense_ctx"].T, np.ones((1, BATCH), np.float32)])
    w2 = a["W_top2"].reshape(HIDDEN1 // P, P, HIDDEN2).transpose(1, 0, 2)

    q = np.arange(P)
    consts = np.concatenate([(1 - q * q)[:, None], np.tile(np.arange(WIDE), (P, 1)),
                             a["b_top2"].reshape(-1, P).T, a["W_top3"].reshape(-1, P).T], axis=1).astype(np.float32)
    quad_w = np.stack([np.full(P, -128), np.full(P, -1), 2 * q]).astype(ml_dtypes.bfloat16)

    arrays = {"ids": ids_all, "tables": tables}
    arrays.update({f"large_{f}": a[f"tbl_{f}"] for f in LARGE})
    arrays.update(consts=consts, selectors=selectors, quad_w=quad_w, w1=w1, w2=w2, dense_t=dense_t)
    arrays = {k: np.ascontiguousarray(v) for k, v in arrays.items()}

    nc = bacc.Bacc("TRN2", target_bir_lowering=False, num_devices=1)
    ap = {k: nc.dram_tensor(k, v.shape, mybir.dt.from_np(v.dtype), kind="ExternalInput").ap()
          for k, v in arrays.items()}
    out = nc.dram_tensor("out", (BATCH, 1), mybir.dt.float32, kind="ExternalOutput").ap()
    build(nc, ap["ids"], ap["tables"], [ap[f"large_{f}"] for f in LARGE], ap["consts"], ap["selectors"],
          ap["quad_w"], ap["w1"], ap["w2"], ap["dense_t"], out)
    result = run_bass_kernel_spmd(nc, [arrays], core_ids=[0])
    return result.results[0]["out"]
```

```python
from contextlib import ExitStack

import numpy as np

import concourse.bass as bass
from concourse import mybir

P = 128
BATCH, NUM_FIELDS, DIM, DENSE = 512, 39, 64, 16
HIDDEN1, HIDDEN2 = 512, 256
TILES = BATCH // P
SPLIT = 3
SET = 32

BLOCKS = {0: 10, 1: 98, 2: 10, 3: 10, 4: 8, 5: 8, 6: 977, 7: 98, 8: 10, 9: 977, 10: 10, 11: 8, 12: 98,
          13: 8, 14: 8, 15: 98, 16: 8, 17: 977, 18: 10, 19: 8, 20: 98, 21: 10, 22: 8, 23: 10, 24: 8,
          25: 10, 26: 8, 27: 10, 28: 8, 29: 98, 30: 10, 31: 8, 32: 10, 33: 98, 34: 10, 35: 10, 36: 8,
          37: 8, 38: 8}
WIDE, NARROW = 10, 8
SMALL = [f for f in range(NUM_FIELDS) if BLOCKS[f] == NARROW] + [f for f in range(NUM_FIELDS) if BLOCKS[f] == WIDE]
LARGE = [f for f in range(NUM_FIELDS) if BLOCKS[f] > WIDE]
NS, NL = len(SMALL), len(LARGE)

GROUPS = [(0, 5, NARROW), (5, 5, NARROW), (10, 5, NARROW), (15, 4, WIDE), (19, 4, WIDE), (23, 3, WIDE), (26, 3, WIDE)]
FIRST_BLOCK = [sum(n * b for _, n, b in GROUPS[:g]) for g in range(len(GROUPS) + 1)]
ALL_BLOCKS = FIRST_BLOCK[-1]
SET_START = [0, 10, 19, NS]
PLACE = {}
for _i, _f in enumerate(SMALL):
    _s = max(s for s in range(3) if SET_START[s] <= _i)
    PLACE[_f] = SET * _s + SPLIT * (_i - SET_START[_s])
for _i, _f in enumerate(LARGE):
    PLACE[_f] = SET * 3 + SPLIT * _i

CHUNK_PAIRS = [105, 128, 128, 128, 128, 124]
CHUNK_ROWS = [CHUNK_PAIRS[0] + DENSE + 1] + CHUNK_PAIRS[1:]
CHUNKS = len(CHUNK_PAIRS)


def chunks_of_pairs():
    small = {f: n for n, f in enumerate(SMALL)}
    late = [GROUPS[g][0] for g in (3, 4, 5, 6)]
    both_small, one_large = [[] for _ in range(5)], [[] for _ in range(5)]
    for i in range(NUM_FIELDS):
        for j in range(i + 1, NUM_FIELDS):
            stage = sum(max(small.get(i, -1), small.get(j, -1)) >= n for n in late)
            (both_small if i in small and j in small else one_large)[stage].append((i, j))
    middle = both_small[1] + both_small[2]
    queue = (both_small[0] + middle[:128] + one_large[0] + one_large[1] + one_large[2] + middle[128:]
             + both_small[3] + one_large[3] + both_small[4] + one_large[4])
    assert len(queue) == sum(CHUNK_PAIRS) == NUM_FIELDS * (NUM_FIELDS - 1) // 2
    return [queue[sum(CHUNK_PAIRS[:c]):sum(CHUNK_PAIRS[:c + 1])] for c in range(CHUNKS)]


QUADS = -(-NS // 2)
EARLY_QUADS = 12
HALF_SUMMED, HALF_WIDTH = (1, 2, 3), 8

STEPS = [((0,), 0, 4), ((2,), 0, 2), ((1,), 0, 4), ((3,), 0, 2), ((2, 3), 2, 3), ((4,), 0, 3), ((5,), 0, 3),
         ((2, 3, 4, 5), 3, 4)]
EARLY = 3
TURNS = [(0, 64, 0, 4), (96, 128, 0, 2), (0, 96, 0, 4), (64, 96, 0, 4), (96, 128, 2, 3), (64, 96, 0, 4),
         (96, 128, 3, 4)]


def build(nc, ids, tables, large, consts, selectors, quad_w, w1, w2, dense_t, out):
    fp32, bf16, i32 = mybir.dt.float32, mybir.dt.bfloat16, mybir.dt.int32
    ALU, ACT, AX = mybir.AluOpType, mybir.ActivationFunctionType, mybir.AxisListType

    with ExitStack() as ctx:
        def sb(name, shape, dt):
            return ctx.enter_context(nc.sbuf_tensor(name, shape, dt))

        def sem(name):
            return ctx.enter_context(nc.semaphore(name))

        n_ids = TILES * NS
        ids_sb = sb("ids_sb", [P, TILES * NL + 2 * n_ids], i32)
        gather_ids = ids_sb[:, 0:TILES * NL]
        block_ids = ids_sb[:, TILES * NL:TILES * NL + n_ids]
        flat_ids = ids_sb[:, TILES * NL + n_ids:]
        block_of = sb("block_of", [P, n_ids], i32)
        row_of = sb("row_of", [P, n_ids], i32)
        row_sq = sb("row_sq", [P, n_ids], i32)
        row_sq_digit = sb("row_sq_digit", [P, 2, n_ids], i32)
        digits = sb("digits", [P, 3, n_ids], bf16)
        query = sb("query", [3, NS * BATCH], bf16)
        quad_w_sb = sb("quad_w_sb", [3, P], bf16)
        consts_sb = sb("consts_sb", [P, 1 + WIDE + 4 + P], fp32)
        one_minus_sq = consts_sb[:, 0:1]
        block_iota = consts_sb[:, 1:1 + WIDE]
        b2_sb = consts_sb[:, 1 + WIDE:3 + WIDE]
        w3_sb = consts_sb[:, 3 + WIDE:5 + WIDE]
        ident_f = consts_sb[:, 5 + WIDE:]
        sel_sb = sb("sel_sb", [P, 2 * CHUNKS + 1, P], bf16)
        ident = sel_sb[:, 2 * CHUNKS, :]
        tables_sb = sb("tables_sb", [P, ALL_BLOCKS, DIM], fp32)
        gathered = sb("gathered", [P, TILES, NL, DIM], fp32)
        row_sums = sb("row_sums", [P, ALL_BLOCKS], fp32)
        row_rest = sb("row_rest", [P, ALL_BLOCKS], fp32)
        row_parts = sb("row_parts", [P, SPLIT * ALL_BLOCKS], bf16)
        large_sums = sb("large_sums", [P, TILES, NL], fp32)
        large_rest = sb("large_rest", [P, TILES, NL], fp32)
        onehot = sb("onehot", [P, NS, BATCH], bf16)
        mask = sb("mask", [P, TILES * ALL_BLOCKS], bf16)
        masked = sb("masked", [P, 2, 512], fp32)
        parts = sb("parts", [P, TILES, P], bf16)
        parts_t = sb("parts_t", [P, BATCH], bf16)
        zeros = sb("zeros", [P, 512], bf16)
        left = sb("left", [P, 2, 512], fp32)
        z = sb("z", [P, CHUNKS, BATCH], fp32)
        w1_sb = sb("w1_sb", [P, CHUNKS, HIDDEN1], fp32)
        w2_sb = sb("w2_sb", [P, HIDDEN1 // P, HIDDEN2], fp32)
        h1 = sb("h1", [P, HIDDEN1 // P, BATCH], fp32)
        h2 = sb("h2", [P, HIDDEN2 // P, BATCH], fp32)
        warm = sb("warm", [P, 1], fp32)
        y = sb("y", [1, BATCH], fp32)

        h1_ps = ctx.enter_context(nc.psum_tensor("h1_ps", [P, HIDDEN1 // P, 512], fp32))
        pair_ps = ctx.enter_context(nc.psum_tensor("pair_ps", [P, 2, 512], fp32))
        look_ps = ctx.enter_context(nc.psum_tensor("look_ps", [P, 512], fp32))
        turn_ps = ctx.enter_context(nc.psum_tensor("turn_ps", [P, 512], fp32))
        turn_bf = [ps.bitcast(bf16) for ps in [turn_ps[:, :]] * (len(TURNS) - 1) + [pair_ps[:, 0, :]]]

        def half_ps(g):
            return pair_ps[:, g % 2, 0:2 * GROUPS[g][2] * HALF_WIDTH].rearrange("p (c w) -> p c w", w=HALF_WIDTH)

        def quad_banks(u):
            return h1_ps[:, 2 * (u % 2):2 * (u % 2) + 2, :] if u < EARLY_QUADS else pair_ps

        h2_ps = [look_ps, turn_ps]
        y_ps = pair_ps[0:1, 1, :]

        ids_loaded = sem("ids_loaded")
        consts_loaded = sem("consts_loaded")
        quad_w_loaded = sem("quad_w_loaded")
        sel_loaded = sem("sel_loaded")
        first_fields_loaded = sem("first_fields_loaded")
        tables_loaded = [sem(f"tables_loaded_{g}") for g in range(len(GROUPS))]
        w1_loaded = [sem(f"w1_loaded_{n}") for n in range(3)]
        w2_loaded = sem("w2_loaded")
        dense_loaded = sem("dense_loaded")
        query_loaded = sem("query_loaded")
        rows_gathered = [sem(f"rows_gathered_{t}") for t in range(TILES)]
        out_stored = sem("out_stored")
        warmup_ready = sem("warmup_ready")
        zeros_set = sem("zeros_set")
        dve_steps = sem("dve_steps")
        digits_ready = sem("digits_ready")
        quads_ready = sem("quads_ready")
        half_summed = sem("half_summed")
        rows_summed = sem("rows_summed")
        onehots_ready = sem("onehots_ready")
        row_parts_ready = sem("row_parts_ready")
        lookups_ready = sem("lookups_ready")
        lookups_masked = sem("lookups_masked")
        small_parts_ready = sem("small_parts_ready")
        large_parts_ready = sem("large_parts_ready")
        turned = sem("turned")
        parts_t_ready = sem("parts_t_ready")
        pairs_selected = sem("pairs_selected")
        left_copied = sem("left_copied")
        z_ready = sem("z_ready")
        layer1_done = sem("layer1_done")
        h1_ready_act = sem("h1_ready_act")
        h1_ready_dve = sem("h1_ready_dve")
        layer2_done = sem("layer2_done")
        h2_ready_act = sem("h2_ready_act")
        h2_ready_dve = sem("h2_ready_dve")
        layer3_done = sem("layer3_done")
        y_ready = sem("y_ready")

        block = ctx.enter_context(nc.Block())

        @block.sync
        def _(sp):
            sp.dma_start(ids_sb[:, :], ids).then_inc(ids_loaded, 16)

            def load_tables(g):
                if g >= 2:
                    sp.wait_ge(tables_loaded[g - 2], 16)
                part = slice(FIRST_BLOCK[g], FIRST_BLOCK[g + 1])
                sp.dma_start(tables_sb[:, part, :], tables[:, part, :]).then_inc(tables_loaded[g], 16)

            def load_w1(n, first, end):
                sp.dma_start(w1_sb[:, first:end, :], w1[:, first:end, :]).then_inc(w1_loaded[n], 16)

            for first, end, loaded in ((0, 2, first_fields_loaded), (2, 5, tables_loaded[0])):
                part = slice(first * NARROW, end * NARROW)
                sp.dma_start(tables_sb[:, part, :], tables[:, part, :]).then_inc(loaded, 16)
            sp.wait_ge(digits_ready, 1)
            for k in range(3):
                sp.dma_start(query[k:k + 1, :].rearrange("k (p n) -> k p n", p=P), digits[:, k, :])\
                  .then_inc(query_loaded, 16)
            load_tables(1)
            load_tables(2)
            load_tables(3)
            sp.dma_start(sel_sb[:, :, :], selectors).then_inc(sel_loaded, 16)
            sp.dma_start(z[CHUNK_PAIRS[0]:CHUNK_ROWS[0], 0, :], dense_t).then_inc(dense_loaded, 16)
            load_w1(0, 0, 1)
            load_tables(4)
            load_w1(1, 1, 4)
            load_tables(5)
            load_w1(2, 4, 6)
            load_tables(6)
            sp.dma_start(w2_sb[:, :, :], w2).then_inc(w2_loaded, 16)
            sp.wait_ge(y_ready, 1)
            sp.dma_start(out.rearrange("b a -> a b"), y[:, :]).then_inc(out_stored, 16)
            sp.wait_ge(out_stored, 16)

        @block.gpsimd
        def _(pool):
            pool.memset(zeros[:, :], 0.0).then_inc(warmup_ready, 1)
            pool.memset(parts[:, :, :], 0.0).then_inc(zeros_set, 1)
            pool.memset(parts_t[:, :], 0.0).then_inc(zeros_set, 1)
            pool.wait_ge(ids_loaded, 16)
            for t in range(TILES):
                for n in range(NL):
                    k = t * NL + n
                    pool.indirect_dma_start(
                        out=gathered[:, t, n, :], out_offset=None, in_=large[n],
                        in_offset=bass.IndirectOffsetOnAxis(ap=gather_ids[:, k:k + 1], axis=0))\
                        .then_inc(rows_gathered[t], 16)

        @block.scalar
        def _(act):
            act.dma_start(consts_sb[:, :], consts).then_inc(consts_loaded, 16)
            act.dma_start(quad_w_sb[:, :], quad_w).then_inc(quad_w_loaded, 16)
            act.wait_ge(consts_loaded, 16)
            nc.scalar.activation(warm[:, :], one_minus_sq, ACT.Relu)
            def make_onehots(first, end):
                for u in range(first, end):
                    fields = min(2, NS - 2 * u)
                    act.wait_ge(quads_ready, u + 1)
                    nc.scalar.activation(onehot[:, 2 * u:2 * u + fields, :], quad_banks(u)[:, 0:fields, :], ACT.Relu,
                                         bias=one_minus_sq).then_inc(onehots_ready, 1)

            def copy_turn(n):
                c0, c1, t0, t1 = TURNS[n]
                act.wait_ge(turned, n + 1)
                if n == 0:
                    act.wait_ge(zeros_set, 2)
                nc.scalar.activation(parts_t[c0:c1, t0 * P:t1 * P], turn_bf[n][c0:c1, t0 * P:t1 * P],
                                     ACT.Copy)\
                  .then_inc(parts_t_ready, 1)

            def copy_left(n):
                chunks, t0, t1 = STEPS[n]
                width = len(chunks) * (t1 - t0) * P
                act.wait_ge(pairs_selected, n + 1)
                if n >= 2:
                    act.wait_ge(z_ready, n - 1)
                nc.scalar.activation(left[:, n % 2, 0:width], pair_ps[:, 0, 0:width], ACT.Copy)\
                  .then_inc(left_copied, 1)

            def relu1(n, t0, t1):
                act.wait_ge(layer1_done, n + 1)
                nc.scalar.activation(h1[:, 0:2, t0 * P:t1 * P], h1_ps[:, 0:2, t0 * P:t1 * P], ACT.Relu)\
                  .then_inc(h1_ready_act, 1)

            def relu2(n, t0, t1):
                act.wait_ge(layer2_done, 2 * n + 1)
                nc.scalar.activation(h2[:, 0, t0 * P:t1 * P], h2_ps[0][:, t0 * P:t1 * P], ACT.Relu,
                                     bias=b2_sb[:, 0:1]).then_inc(h2_ready_act, 1)

            make_onehots(0, EARLY_QUADS)
            copy_turn(0)
            copy_left(0)
            make_onehots(EARLY_QUADS, QUADS)
            copy_turn(1)
            copy_left(1)
            copy_turn(2)
            copy_left(2)
            copy_left(3)
            copy_turn(3)
            copy_turn(4)
            copy_left(4)
            copy_left(5)
            copy_turn(5)
            copy_left(6)
            copy_turn(6)
            relu1(0, 0, EARLY)
            copy_left(7)
            relu2(0, 0, EARLY)
            relu1(1, EARLY, TILES)
            relu2(1, EARLY, TILES)

        @block.tensor
        def _(pe):
            def quads(first, end):
                for u in range(first, end):
                    if u >= 2:
                        pe.wait_ge(onehots_ready, u - 1 if u < EARLY_QUADS else u)
                    for f in range(2 * u, min(2 * u + 2, NS)):
                        last = nc.tensor.matmul(quad_banks(u)[:, f % 2, :], quad_w_sb[:, :],
                                                query[:, f * BATCH:(f + 1) * BATCH], start=True, stop=True)
                    last.then_inc(quads_ready, 1)
                    if u < EARLY_QUADS:
                        keep_warm(2)

            def half_sum(g):
                b = FIRST_BLOCK[g + 1]
                a = b - 2 * GROUPS[g][2]
                pe.wait_ge(tables_loaded[g], 16)
                if g >= 3:
                    pe.wait_ge(rows_summed, g - 2)
                for k in range(DIM // HALF_WIDTH):
                    last = nc.tensor.matmul(half_ps(g), ident_f,
                                            tables_sb[:, a:b, k * HALF_WIDTH:(k + 1) * HALF_WIDTH],
                                            start=(k == 0), stop=(k == DIM // HALF_WIDTH - 1))
                last.then_inc(half_summed, 1)

            def keep_warm(n):
                for _ in range(n):
                    nc.tensor.matmul(turn_ps[:, :], zeros[:, 0:P], zeros[:, :], start=True, stop=True)

            def lookups(g):
                first, count, blocks = GROUPS[g]
                n = SPLIT * blocks
                pe.wait_ge(row_parts_ready, g + 1)
                pe.wait_ge(onehots_ready, (first + count + 1) // 2)
                if g >= 1:
                    pe.wait_ge(lookups_masked, g)
                for t in range(TILES):
                    for f in range(count):
                        at = (t * count + f) * n
                        src = SPLIT * FIRST_BLOCK[g] + f * n
                        last = nc.tensor.matmul(look_ps[:, at:at + n], onehot[:, first + f, t * P:(t + 1) * P],
                                                row_parts[:, src:src + n], start=True, stop=True)
                last.then_inc(lookups_ready, 1)

            def turn(n):
                c0, c1, t0, t1 = TURNS[n]
                for t in range(t0, t1):
                    last = nc.tensor.transpose(turn_bf[n][c0:c1, t * P:(t + 1) * P], parts[:, t, c0:c1], ident)
                last.then_inc(turned, 1)

            def select(n):
                chunks, t0, t1 = STEPS[n]
                w = (t1 - t0) * P
                rows = {0: 64, 2: 96}.get(n, P)
                if n >= 1:
                    pe.wait_ge(z_ready, n)
                for side in range(2):
                    for i, c in enumerate(chunks):
                        last = nc.tensor.matmul(pair_ps[:, side, i * w:(i + 1) * w], sel_sb[0:rows, 2 * c + side, :],
                                                parts_t[0:rows, t0 * P:t1 * P], start=True, stop=True)
                last.then_inc(pairs_selected, 1)

            def layer1(n, between=lambda m: None):
                chunks, t0, t1 = STEPS[n]
                pe.wait_ge(z_ready, n + 1)
                for c in chunks:
                    rows = CHUNK_ROWS[c]
                    for m in range(HIDDEN1 // P):
                        last = nc.tensor.matmul(h1_ps[:, m, t0 * P:t1 * P], w1_sb[0:rows, c, m * P:(m + 1) * P],
                                                z[0:rows, c, t0 * P:t1 * P], start=(n == 0), stop=(c == CHUNKS - 1),
                                                skip_group_check=True)
                        between(m)
                if CHUNKS - 1 in chunks:
                    last.then_inc(layer1_done, 1)

            def layer2(n, t0, t1):
                pe.wait_ge(h1_ready_act, n + 1)
                for m in range(HIDDEN2 // P):
                    for k in range(HIDDEN1 // P):
                        if m == 0 and k == 2:
                            pe.wait_ge(h1_ready_dve, n + 1)
                        last = nc.tensor.matmul(h2_ps[m][:, t0 * P:t1 * P], w2_sb[:, k, m * P:(m + 1) * P],
                                                h1[:, k, t0 * P:t1 * P], start=(k == 0), stop=(k == HIDDEN1 // P - 1))
                    last.then_inc(layer2_done, 1)

            def layer3(n, t0, t1):
                for k in range(HIDDEN2 // P):
                    pe.wait_ge(h2_ready_act if k == 0 else h2_ready_dve, n + 1)
                    last = nc.tensor.matmul(y_ps[:, t0 * P:t1 * P], w3_sb[:, k:k + 1],
                                            h2[:, k, t0 * P:t1 * P], start=(k == 0), stop=(k == HIDDEN2 // P - 1))
                last.then_inc(layer3_done, 1)

            pe.wait_ge(warmup_ready, 1)
            keep_warm(20)
            pe.wait_ge(quad_w_loaded, 16)
            pe.wait_ge(query_loaded, 3 * 16)
            quads(0, 5)
            lookups(0)
            half_sum(1)
            quads(5, 8)
            lookups(1)
            half_sum(2)
            quads(8, EARLY_QUADS)
            lookups(2)
            half_sum(3)
            pe.wait_ge(sel_loaded, 16)
            pe.wait_ge(small_parts_ready, 3)
            turn(0)
            pe.wait_ge(parts_t_ready, 1)
            pe.wait_ge(rows_summed, 3)
            select(0)
            keep_warm(6)
            pe.wait_ge(z_ready, 1)
            quads(EARLY_QUADS, EARLY_QUADS + 1)
            pe.wait_ge(w1_loaded[0], 16)
            pe.wait_ge(dense_loaded, 16)
            pe.wait_ge(onehots_ready, EARLY_QUADS)
            layer1(0, lambda m: (quads(EARLY_QUADS + 1 + m, min(EARLY_QUADS + 2 + m, QUADS)), m == 0 and lookups(3)))
            pe.wait_ge(large_parts_ready, 2)
            turn(1)
            pe.wait_ge(onehots_ready, QUADS)
            pe.wait_ge(parts_t_ready, 2)
            select(1)
            lookups(4)
            pe.wait_ge(small_parts_ready, 5)
            turn(2)
            pe.wait_ge(parts_t_ready, 3)
            select(2)
            pe.wait_ge(w1_loaded[1], 16)
            layer1(1)
            lookups(5)
            select(3)
            layer1(2)
            pe.wait_ge(small_parts_ready, 6)
            turn(3)
            pe.wait_ge(large_parts_ready, 3)
            turn(4)
            pe.wait_ge(parts_t_ready, 5)
            select(4)
            layer1(3)
            lookups(6)
            select(5)
            layer1(4)
            pe.wait_ge(small_parts_ready, 7)
            turn(5)
            pe.wait_ge(parts_t_ready, 6)
            select(6)
            pe.wait_ge(w1_loaded[2], 16)
            layer1(5)
            layer1(6)
            pe.wait_ge(large_parts_ready, 4)
            turn(6)
            pe.wait_ge(parts_t_ready, 7)
            select(7)
            pe.wait_ge(w2_loaded, 16)
            layer2(0, 0, EARLY)
            layer1(7)
            layer3(0, 0, EARLY)
            layer2(1, EARLY, TILES)
            layer3(1, EARLY, TILES)

        @block.vector
        def _(dve):
            chain = [0]

            def link(instruction):
                chain[0] += 1
                instruction.then_inc(dve_steps, 1)
                dve.wait_ge(dve_steps, chain[0])

            def split(total, rest, hi, mid, lo, done, between=(lambda: None, lambda: None)):
                nc.vector.tensor_copy(hi, total).then_inc(dve_steps, 1)
                chain[0] += 1
                after_hi = chain[0]
                between[0]()
                dve.wait_ge(dve_steps, after_hi)
                nc.vector.tensor_tensor(rest, total, hi, ALU.subtract).then_inc(dve_steps, 1)
                chain[0] += 1
                after_rest = chain[0]
                between[1]()
                dve.wait_ge(dve_steps, after_rest)
                link(nc.vector.tensor_copy(mid, rest))
                nc.vector.tensor_tensor(lo, rest, mid, ALU.subtract).then_inc(done, 1)

            def sum_rows(g):
                a, b = FIRST_BLOCK[g], FIRST_BLOCK[g + 1]
                split_at = b - 2 * GROUPS[g][2] if g in HALF_SUMMED else b
                if g == 0:
                    a = 2 * NARROW
                    dve.wait_ge(first_fields_loaded, 16)
                    nc.vector.tensor_reduce(row_sums[:, 0:a], tables_sb[:, 0:a, :], op=ALU.add, axis=AX.X)
                dve.wait_ge(tables_loaded[g], 16)
                link(nc.vector.tensor_reduce(row_sums[:, a:split_at], tables_sb[:, a:split_at, :], op=ALU.add, axis=AX.X))
                if g in HALF_SUMMED:
                    dve.wait_ge(half_summed, g)
                    nc.vector.tensor_reduce(row_sums[:, split_at:b], half_ps(g), op=ALU.add, axis=AX.X)\
                      .then_inc(rows_summed, 1)
                    dve.wait_ge(rows_summed, g)

            def split_rows(g, between=(lambda: None, lambda: None)):
                _, count, blocks = GROUPS[g]
                a, b = FIRST_BLOCK[g], FIRST_BLOCK[g + 1]
                by_part = row_parts[:, SPLIT * a:SPLIT * b].rearrange("p (f s c) -> p f s c", s=SPLIT, c=blocks)
                split(row_sums[:, a:b].rearrange("p (f c) -> p f c", c=blocks),
                      row_rest[:, a:b].rearrange("p (f c) -> p f c", c=blocks),
                      by_part[:, :, 0, :], by_part[:, :, 1, :], by_part[:, :, 2, :], row_parts_ready, between)

            def keep_block(g):
                _, count, blocks = GROUPS[g]
                n = TILES * count
                keep = mask[:, TILES * FIRST_BLOCK[g]:TILES * FIRST_BLOCK[g + 1]].rearrange("p (n c) -> p n c", c=blocks)
                dve.wait_ge(lookups_ready, g + 1)
                nc.vector.tensor_tensor(
                    masked[:, g % 2, 0:n * SPLIT * blocks].rearrange("p (n s c) -> p n s c", s=SPLIT, c=blocks),
                    look_ps[:, 0:n * SPLIT * blocks].rearrange("p (n s c) -> p n s c", s=SPLIT, c=blocks),
                    keep.unsqueeze(2).to_broadcast([P, n, SPLIT, blocks]), ALU.mult).then_inc(lookups_masked, 1)

            def sum_blocks(g):
                first, count, blocks = GROUPS[g]
                place = PLACE[SMALL[first]]
                dve.wait_ge(lookups_masked, g + 1)
                if g in (3, 5, 6):
                    dve.wait_ge(turned, {3: 1, 5: 3, 6: 4}[g])
                with nc.allow_low_precision(reason="a sum of one bfloat16 value and zeros is exact"):
                    nc.vector.tensor_reduce(
                        parts[:, :, place:place + SPLIT * count],
                        masked[:, g % 2, 0:TILES * count * SPLIT * blocks]
                        .rearrange("p (t m c) -> p t m c", t=TILES, c=blocks),
                        op=ALU.add, axis=AX.X).then_inc(small_parts_ready, 1)

            def large_parts(t):
                dve.wait_ge(rows_gathered[t], NL * 16)
                link(nc.vector.tensor_reduce(large_sums[:, t, :], gathered[:, t, :, :], op=ALU.add, axis=AX.X))
                by_part = parts[:, t, 3 * SET:3 * SET + SPLIT * NL].rearrange("p (f s) -> p f s", s=SPLIT)
                split(large_sums[:, t, :], large_rest[:, t, :], by_part[:, :, 0], by_part[:, :, 1], by_part[:, :, 2],
                      large_parts_ready)

            def multiply_pairs(n):
                chunks, t0, t1 = STEPS[n]
                w = (t1 - t0) * P
                rows = min(CHUNK_PAIRS[c] for c in chunks) if len(chunks) == 1 else P
                cols = slice(0, len(chunks) * w)
                dve.wait_ge(left_copied, n + 1)
                nc.vector.tensor_tensor(
                    z[0:rows, chunks[0]:chunks[0] + len(chunks), t0 * P:t1 * P],
                    pair_ps[0:rows, 1, cols].rearrange("p (c w) -> p c w", w=w),
                    left[0:rows, n % 2, cols].rearrange("p (c w) -> p c w", w=w), ALU.mult).then_inc(z_ready, 1)

            def relu1(n, t0, t1):
                dve.wait_ge(layer1_done, n + 1)
                nc.vector.tensor_scalar(h1[:, 2:4, t0 * P:t1 * P], h1_ps[:, 2:4, t0 * P:t1 * P], 0.0, None, ALU.max)\
                  .then_inc(h1_ready_dve, 1)

            def relu2(n, t0, t1):
                dve.wait_ge(layer2_done, 2 * n + 2)
                nc.vector.tensor_scalar(h2[:, 1, t0 * P:t1 * P], h2_ps[1][:, t0 * P:t1 * P], b2_sb[:, 1:2], 0.0,
                                        ALU.add, ALU.max).then_inc(h2_ready_dve, 1)

            dve.wait_ge(ids_loaded, 16)
            link(nc.vector.tensor_scalar(row_of[:, :], flat_ids, P - 1, None, ALU.bitwise_and))
            nc.vector.tensor_copy(digits[:, 2, :], row_of[:, :])
            link(nc.vector.tensor_tensor(row_sq[:, :], row_of[:, :], row_of[:, :], ALU.mult))
            nc.vector.tensor_scalar(row_sq_digit[:, 0, :], row_sq[:, :], 7, None, ALU.logical_shift_right)
            link(nc.vector.tensor_scalar(row_sq_digit[:, 1, :], row_sq[:, :], P - 1, None, ALU.bitwise_and))
            nc.vector.tensor_copy(digits[:, 0:2, :], row_sq_digit[:, :, :]).then_inc(digits_ready, 1)
            link(nc.vector.tensor_scalar(block_of[:, :], block_ids, 7, None, ALU.logical_shift_right))
            dve.wait_ge(consts_loaded, 16)
            for g0, g1 in ((0, 3), (3, len(GROUPS))):
                a, b, blocks = GROUPS[g0][0], GROUPS[g1 - 1][0] + GROUPS[g1 - 1][1], GROUPS[g0][2]
                n = TILES * (b - a)
                at = TILES * FIRST_BLOCK[g0]
                link(nc.vector.tensor_tensor(
                    mask[:, at:at + n * blocks].rearrange("p (n c) -> p n c", c=blocks),
                    block_of[:, TILES * a:TILES * b].unsqueeze(2).to_broadcast([P, n, blocks]),
                    block_iota[:, 0:blocks].unsqueeze(1).to_broadcast([P, n, blocks]), ALU.is_equal))
            dve.wait_ge(zeros_set, 2)
            sum_rows(0)
            split_rows(0)
            sum_rows(1)
            split_rows(1, (lambda: keep_block(0), lambda: sum_blocks(0)))
            sum_rows(2)
            split_rows(2, (lambda: keep_block(1), lambda: sum_blocks(1)))
            large_parts(0)
            keep_block(2)
            sum_blocks(2)
            sum_rows(3)
            multiply_pairs(0)
            split_rows(3)
            sum_rows(4)
            split_rows(4, (lambda: keep_block(3), lambda: sum_blocks(3)))
            large_parts(1)
            sum_rows(5)
            multiply_pairs(1)
            split_rows(5, (lambda: keep_block(4), lambda: sum_blocks(4)))
            sum_rows(6)
            multiply_pairs(2)
            split_rows(6, (lambda: keep_block(5), lambda: sum_blocks(5)))
            multiply_pairs(3)
            large_parts(2)
            keep_block(6)
            sum_blocks(6)
            multiply_pairs(4)
            multiply_pairs(5)
            multiply_pairs(6)
            large_parts(3)
            relu1(0, 0, EARLY)
            multiply_pairs(7)
            relu2(0, 0, EARLY)
            relu1(1, EARLY, TILES)
            relu2(1, EARLY, TILES)
            dve.wait_ge(layer3_done, 2)
            nc.vector.tensor_copy(y[:, :], y_ps).then_inc(y_ready, 1)


def kernel(**inputs):
    import ml_dtypes
    import concourse.bacc as bacc
    from concourse.bass_utils import run_bass_kernel_spmd

    a = {k: np.asarray(v) for k, v in inputs.items()}
    for f in range(NUM_FIELDS):
        assert -(-a[f"tbl_{f}"].shape[0] // P) == BLOCKS[f]

    ids = a["ids"]
    by_tile = ids.reshape(TILES, P, NUM_FIELDS).transpose(1, 0, 2)
    ids_all = np.concatenate(
        [by_tile[:, :, LARGE].reshape(P, -1)]
        + [by_tile[:, :, SMALL[s:s + n]].reshape(P, -1) for s, n, _ in GROUPS]
        + [np.ascontiguousarray(ids[:, SMALL].T).reshape(P, -1)], axis=1)

    def blocked(f):
        rows = a[f"tbl_{f}"]
        padded = np.zeros((BLOCKS[f] * P, DIM), rows.dtype)
        padded[:rows.shape[0]] = rows
        return padded.reshape(BLOCKS[f], P, DIM).transpose(1, 0, 2)

    tables = np.concatenate([blocked(f) for f in SMALL], axis=1)

    chunks = chunks_of_pairs()
    number = {}
    for i in range(NUM_FIELDS):
        for j in range(i + 1, NUM_FIELDS):
            number[i, j] = len(number)
    w1 = np.zeros((P, CHUNKS, HIDDEN1), np.float32)
    selectors = np.zeros((P, 2 * CHUNKS + 1, P), ml_dtypes.bfloat16)
    for c, pairs in enumerate(chunks):
        w1[:len(pairs), c] = a["W_top1"][[number[p] for p in pairs]]
        for r, pair in enumerate(pairs):
            for side in range(2):
                selectors[PLACE[pair[side]]:PLACE[pair[side]] + SPLIT, 2 * c + side, r] = 1
    selectors[:, 2 * CHUNKS] = np.eye(P)
    w1[CHUNK_PAIRS[0]:CHUNK_ROWS[0] - 1, 0] = a["W_top1"][len(number):]
    w1[CHUNK_ROWS[0] - 1, 0] = a["b_top1"]
    dense_t = np.concatenate([a["dense_ctx"].T, np.ones((1, BATCH), np.float32)])
    w2 = a["W_top2"].reshape(HIDDEN1 // P, P, HIDDEN2).transpose(1, 0, 2)

    q = np.arange(P)
    consts = np.concatenate([(1 - q * q)[:, None], np.tile(np.arange(WIDE), (P, 1)),
                             a["b_top2"].reshape(-1, P).T, a["W_top3"].reshape(-1, P).T, np.eye(P)],
                            axis=1).astype(np.float32)
    quad_w = np.stack([np.full(P, -128), np.full(P, -1), 2 * q]).astype(ml_dtypes.bfloat16)

    arrays = {"ids": ids_all, "tables": tables}
    arrays.update({f"large_{f}": a[f"tbl_{f}"] for f in LARGE})
    arrays.update(consts=consts, selectors=selectors, quad_w=quad_w, w1=w1, w2=w2, dense_t=dense_t)
    arrays = {k: np.ascontiguousarray(v) for k, v in arrays.items()}

    nc = bacc.Bacc("TRN2", target_bir_lowering=False, num_devices=1)
    ap = {k: nc.dram_tensor(k, v.shape, mybir.dt.from_np(v.dtype), kind="ExternalInput").ap()
          for k, v in arrays.items()}
    out = nc.dram_tensor("out", (BATCH, 1), mybir.dt.float32, kind="ExternalOutput").ap()
    build(nc, ap["ids"], ap["tables"], [ap[f"large_{f}"] for f in LARGE], ap["consts"], ap["selectors"],
          ap["quad_w"], ap["w1"], ap["w2"], ap["dense_t"], out)
    result = run_bass_kernel_spmd(nc, [arrays], core_ids=[0])
    return result.results[0]["out"]
```

```python
from contextlib import ExitStack

import numpy as np

import concourse.bass as bass
from concourse import mybir

P = 128
BATCH, NUM_FIELDS, DIM, DENSE = 512, 39, 64, 16
HIDDEN1, HIDDEN2 = 512, 256
TILES = BATCH // P
SPLIT = 3
SET = 32

BLOCKS = {0: 10, 1: 98, 2: 10, 3: 10, 4: 8, 5: 8, 6: 977, 7: 98, 8: 10, 9: 977, 10: 10, 11: 8, 12: 98,
          13: 8, 14: 8, 15: 98, 16: 8, 17: 977, 18: 10, 19: 8, 20: 98, 21: 10, 22: 8, 23: 10, 24: 8,
          25: 10, 26: 8, 27: 10, 28: 8, 29: 98, 30: 10, 31: 8, 32: 10, 33: 98, 34: 10, 35: 10, 36: 8,
          37: 8, 38: 8}
WIDE, NARROW = 10, 8
SMALL = [f for f in range(NUM_FIELDS) if BLOCKS[f] == NARROW] + [f for f in range(NUM_FIELDS) if BLOCKS[f] == WIDE]
LARGE = [f for f in range(NUM_FIELDS) if BLOCKS[f] > WIDE]
NS, NL = len(SMALL), len(LARGE)

GROUPS = [(0, 5, NARROW), (5, 5, NARROW), (10, 5, NARROW), (15, 4, WIDE), (19, 4, WIDE), (23, 3, WIDE), (26, 3, WIDE)]
FIRST_BLOCK = [sum(n * b for _, n, b in GROUPS[:g]) for g in range(len(GROUPS) + 1)]
ALL_BLOCKS = FIRST_BLOCK[-1]
SET_START = [0, 10, 19, NS]
PLACE = {}
for _i, _f in enumerate(SMALL):
    _s = max(s for s in range(3) if SET_START[s] <= _i)
    PLACE[_f] = SET * _s + SPLIT * (_i - SET_START[_s])
for _i, _f in enumerate(LARGE):
    PLACE[_f] = SET * 3 + SPLIT * _i

CHUNK_PAIRS = [105, 128, 128, 128, 128, 124]
CHUNK_ROWS = [CHUNK_PAIRS[0] + DENSE + 1] + CHUNK_PAIRS[1:]
CHUNKS = len(CHUNK_PAIRS)


def chunks_of_pairs():
    small = {f: n for n, f in enumerate(SMALL)}
    late = [GROUPS[g][0] for g in (3, 4, 5, 6)]
    both_small, one_large = [[] for _ in range(5)], [[] for _ in range(5)]
    for i in range(NUM_FIELDS):
        for j in range(i + 1, NUM_FIELDS):
            stage = sum(max(small.get(i, -1), small.get(j, -1)) >= n for n in late)
            (both_small if i in small and j in small else one_large)[stage].append((i, j))
    middle = both_small[1] + both_small[2]
    queue = (both_small[0] + middle[:128] + one_large[0] + one_large[1] + one_large[2] + middle[128:]
             + both_small[3] + one_large[3] + both_small[4] + one_large[4])
    assert len(queue) == sum(CHUNK_PAIRS) == NUM_FIELDS * (NUM_FIELDS - 1) // 2
    return [queue[sum(CHUNK_PAIRS[:c]):sum(CHUNK_PAIRS[:c + 1])] for c in range(CHUNKS)]


QUADS = -(-NS // 2)
HALF_SUMMED, HALF_WIDTH = {1: (3, 5), 2: (3, 5), 3: (2, 4), 4: (0, 1)}, 8
ACT_SUMMED = {4: [3], 5: [0], 6: [0]}

STEPS = [((0,), 0, 4), ((2,), 0, 2), ((1,), 0, 2), ((1,), 2, 4), ((3,), 0, 2), ((2, 3), 2, 3), ((4,), 0, 3),
         ((5,), 0, 3), ((2, 3, 4, 5), 3, 4)]
SELECTOR = {c: 1 + 2 * n for n, c in enumerate(dict.fromkeys(c for chunks, _, _ in STEPS for c in chunks))}
FIRST_SELECTORS = 5
HALVES = 2
TURNS = [(0, 64, 0, 4), (96, 128, 0, 2), (0, 96, 0, 4), (96, 128, 2, 3), (64, 96, 0, 4), (64, 96, 0, 4),
         (96, 128, 3, 4)]


def build(nc, ids, tables, large, consts, selectors, quad_w, w1, w2, dense_t, out):
    fp32, bf16, i32 = mybir.dt.float32, mybir.dt.bfloat16, mybir.dt.int32
    ALU, ACT, AX = mybir.AluOpType, mybir.ActivationFunctionType, mybir.AxisListType

    with ExitStack() as ctx:
        def sb(name, shape, dt):
            return ctx.enter_context(nc.sbuf_tensor(name, shape, dt))

        def sem(name):
            return ctx.enter_context(nc.semaphore(name))

        n_ids = TILES * NS
        ids_sb = sb("ids_sb", [P, TILES * NL + 2 * n_ids], i32)
        gather_ids = ids_sb[:, 0:TILES * NL]
        block_ids = ids_sb[:, TILES * NL:TILES * NL + n_ids]
        flat_ids = ids_sb[:, TILES * NL + n_ids:]
        block_of = sb("block_of", [P, n_ids], i32)
        row_of = sb("row_of", [P, n_ids], i32)
        row_sq = sb("row_sq", [P, n_ids], i32)
        row_sq_digit = sb("row_sq_digit", [P, 2, n_ids], i32)
        digits = sb("digits", [P, 3, n_ids], bf16)
        query = sb("query", [3, NS * BATCH], bf16)
        quad_w_sb = sb("quad_w_sb", [3, P], bf16)
        consts_sb = sb("consts_sb", [P, 1 + WIDE + 4 + P], fp32)
        one_minus_sq = consts_sb[:, 0:1]
        block_iota = consts_sb[:, 1:1 + WIDE]
        b2_sb = consts_sb[:, 1 + WIDE:3 + WIDE]
        w3_sb = consts_sb[:, 3 + WIDE:5 + WIDE]
        ident_f = consts_sb[:, 5 + WIDE:]
        sel_sb = sb("sel_sb", [P, 2 * CHUNKS + 1, P], bf16)
        ident = sel_sb[:, 0, :]
        tables_sb = sb("tables_sb", [P, ALL_BLOCKS, DIM], fp32)
        gathered = sb("gathered", [P, TILES, NL, DIM], fp32)
        row_sums = sb("row_sums", [P, ALL_BLOCKS], fp32)
        row_rest = sb("row_rest", [P, ALL_BLOCKS], fp32)
        row_parts = sb("row_parts", [P, SPLIT * ALL_BLOCKS], bf16)
        large_sums = sb("large_sums", [P, TILES, NL], fp32)
        large_rest = sb("large_rest", [P, TILES, NL], fp32)
        onehot = sb("onehot", [P, NS, BATCH], bf16)
        mask = sb("mask", [P, TILES * ALL_BLOCKS], bf16)
        masked = sb("masked", [P, 2, 512], fp32)
        parts = sb("parts", [P, TILES, P], bf16)
        parts_t = sb("parts_t", [P, BATCH], bf16)
        zeros = sb("zeros", [P, 512], bf16)
        left = sb("left", [P, 2, 512], fp32)
        z = sb("z", [P, CHUNKS, BATCH], fp32)
        w1_sb = sb("w1_sb", [P, CHUNKS, HIDDEN1], fp32)
        w2_sb = sb("w2_sb", [P, HIDDEN1 // P, HIDDEN2], fp32)
        h1 = sb("h1", [P, HIDDEN1 // P, BATCH], fp32)
        h2 = sb("h2", [P, HIDDEN2 // P, BATCH], fp32)
        warm = sb("warm", [P, 1], fp32)
        y = sb("y", [1, BATCH], fp32)

        h1_ps = ctx.enter_context(nc.psum_tensor("h1_ps", [P, HIDDEN1 // P, 512], fp32))
        pair_ps = ctx.enter_context(nc.psum_tensor("pair_ps", [P, 2, 512], fp32))
        look_ps = ctx.enter_context(nc.psum_tensor("look_ps", [P, 512], fp32))
        turn_ps = ctx.enter_context(nc.psum_tensor("turn_ps", [P, 512], fp32))
        turn_bf = turn_ps[:, :].bitcast(bf16)

        def half_blocks(g):
            return [FIRST_BLOCK[g] + f * GROUPS[g][2] for f in HALF_SUMMED[g]]

        def half_ps(g):
            a, b = half_blocks(g)
            bank = h1_ps[:, 3, :] if g == 4 else pair_ps[:, g % 2, :]
            return bank[:, 0:(b - a) * HALF_WIDTH].rearrange("p (c w) -> p c w", w=HALF_WIDTH)

        def quad_banks(u):
            return h1_ps[:, 2 * (u % 2):2 * (u % 2) + 2, :]

        h2_ps = [look_ps, turn_ps]
        y_ps = h1_ps[0:1, 0:HALVES, 0:BATCH // HALVES]

        ids_loaded = sem("ids_loaded")
        consts_loaded = sem("consts_loaded")
        quad_w_loaded = sem("quad_w_loaded")
        sel_loaded = [sem(f"sel_loaded_{n}") for n in range(2)]
        tables_loaded = [[sem(f"tables_loaded_{g}_{half}") for half in range(2)] for g in range(len(GROUPS))]
        w1_loaded = [sem(f"w1_loaded_{c}") for c in range(CHUNKS)]
        w2_loaded = sem("w2_loaded")
        dense_loaded = sem("dense_loaded")
        query_loaded = sem("query_loaded")
        rows_gathered = [sem(f"rows_gathered_{t}") for t in range(TILES)]
        out_stored = sem("out_stored")
        warmup_ready = sem("warmup_ready")
        zeros_set = sem("zeros_set")
        dve_steps = sem("dve_steps")
        digits_ready = sem("digits_ready")
        quads_ready = sem("quads_ready")
        half_summed = sem("half_summed")
        rows_summed = sem("rows_summed")
        rows_summed_act = sem("rows_summed_act")
        onehots_ready = sem("onehots_ready")
        row_parts_ready = sem("row_parts_ready")
        lookups_ready = sem("lookups_ready")
        lookups_masked = sem("lookups_masked")
        small_parts_ready = sem("small_parts_ready")
        large_parts_ready = sem("large_parts_ready")
        turned = sem("turned")
        parts_t_ready = sem("parts_t_ready")
        pairs_selected = sem("pairs_selected")
        left_copied = sem("left_copied")
        z_ready = sem("z_ready")
        layer1_done = sem("layer1_done")
        h1_ready = [sem(f"h1_ready_{m}") for m in range(HIDDEN1 // P)]
        layer2_done = sem("layer2_done")
        h2_ready = [sem(f"h2_ready_{m}") for m in range(HIDDEN2 // P)]
        layer3_done = sem("layer3_done")
        y_ready = sem("y_ready")

        block = ctx.enter_context(nc.Block())

        @block.sync
        def _(sp):
            sp.dma_start(ids_sb[:, :], ids).then_inc(ids_loaded, 16)

            issued = []

            def load(dst, src, loaded):
                if len(issued) >= 3:
                    sp.wait_ge(issued[-3], 16)
                sp.dma_start(dst, src).then_inc(loaded, 16)
                issued.append(loaded)

            def load_tables(g):
                (_, count, blocks), a = GROUPS[g], FIRST_BLOCK[g]
                middle = a + count // 2 * blocks
                for n, part in enumerate((slice(a, middle), slice(middle, FIRST_BLOCK[g + 1]))):
                    load(tables_sb[:, part, :], tables[:, part, :], tables_loaded[g][n])

            def load_w1(c):
                load(w1_sb[:, c, :], w1[:, c, :], w1_loaded[c])

            load_tables(0)
            sp.wait_ge(digits_ready, 1)
            for k in range(3):
                sp.dma_start(query[k:k + 1, :].rearrange("k (p n) -> k p n", p=P), digits[:, k, :])\
                  .then_inc(query_loaded, 16)
            load_tables(1)
            load_tables(2)
            load_tables(3)
            load(sel_sb[:, 0:FIRST_SELECTORS, :], selectors[:, 0:FIRST_SELECTORS, :], sel_loaded[0])
            load(z[CHUNK_PAIRS[0]:CHUNK_ROWS[0], 0, :], dense_t, dense_loaded)
            load_w1(0)
            load_tables(4)
            load(sel_sb[:, FIRST_SELECTORS:, :], selectors[:, FIRST_SELECTORS:, :], sel_loaded[1])
            load_w1(2)
            load_tables(5)
            load_w1(1)
            load_tables(6)
            for c in range(3, CHUNKS):
                load_w1(c)
            load(w2_sb[:, :, :], w2, w2_loaded)
            sp.wait_ge(y_ready, 2)
            sp.dma_start(out.rearrange("b a -> a b"), y[:, :]).then_inc(out_stored, 16)
            sp.wait_ge(out_stored, 16)

        @block.gpsimd
        def _(pool):
            pool.memset(zeros[:, :], 0.0).then_inc(warmup_ready, 1)
            pool.memset(parts[:, :, :], 0.0).then_inc(zeros_set, 1)
            pool.memset(parts_t[:, :], 0.0).then_inc(zeros_set, 1)
            pool.wait_ge(ids_loaded, 16)
            for t in range(TILES):
                for n in range(NL):
                    k = t * NL + n
                    pool.indirect_dma_start(
                        out=gathered[:, t, n, :], out_offset=None, in_=large[n],
                        in_offset=bass.IndirectOffsetOnAxis(ap=gather_ids[:, k:k + 1], axis=0))\
                        .then_inc(rows_gathered[t], 16)

        @block.scalar
        def _(act):
            act.dma_start(consts_sb[:, :], consts).then_inc(consts_loaded, 16)
            act.dma_start(quad_w_sb[:, :], quad_w).then_inc(quad_w_loaded, 16)
            act.wait_ge(consts_loaded, 16)
            nc.scalar.activation(warm[:, :], one_minus_sq, ACT.Relu)
            def make_onehots(first, end):
                for u in range(first, end):
                    fields = min(2, NS - 2 * u)
                    act.wait_ge(quads_ready, u + 1)
                    nc.scalar.activation(onehot[:, 2 * u:2 * u + fields, :], quad_banks(u)[:, 0:fields, :], ACT.Relu,
                                         bias=one_minus_sq).then_inc(onehots_ready, 1)

            def sum_field_rows(g, f):
                _, count, blocks = GROUPS[g]
                act.wait_ge(tables_loaded[g][f >= count // 2], 16)
                for c in range(FIRST_BLOCK[g] + f * blocks, FIRST_BLOCK[g] + (f + 1) * blocks):
                    last = nc.scalar.activation(tables_sb[:, c, :], tables_sb[:, c, :], ACT.Copy,
                                                accum_out=row_sums[:, c:c + 1])
                last.then_inc(rows_summed_act, 1)

            def copy_turn(n):
                c0, c1, t0, t1 = TURNS[n]
                act.wait_ge(turned, n + 1)
                if n == 0:
                    act.wait_ge(zeros_set, 2)
                nc.scalar.activation(parts_t[c0:c1, t0 * P:t1 * P], turn_bf[c0:c1, t0 * P:t1 * P],
                                     ACT.Copy)\
                  .then_inc(parts_t_ready, 1)

            def copy_left(n):
                chunks, t0, t1 = STEPS[n]
                width = len(chunks) * (t1 - t0) * P
                act.wait_ge(pairs_selected, n + 1)
                if n >= 2:
                    act.wait_ge(z_ready, n - 1)
                nc.scalar.activation(left[:, n % 2, 0:width], pair_ps[:, 0, 0:width], ACT.Copy)\
                  .then_inc(left_copied, 1)

            def relu1(m):
                act.wait_ge(layer1_done, m + 1)
                nc.scalar.activation(h1[:, m, :], h1_ps[:, m, :], ACT.Relu).then_inc(h1_ready[m], 1)

            make_onehots(0, 14)
            copy_turn(0)
            make_onehots(14, QUADS)
            copy_left(0)
            sum_field_rows(4, 3)
            copy_turn(1)
            copy_left(1)
            sum_field_rows(5, 0)
            copy_turn(2)
            copy_left(2)
            copy_left(3)
            sum_field_rows(6, 0)
            copy_left(4)
            copy_turn(3)
            copy_left(5)
            copy_turn(4)
            copy_left(6)
            copy_turn(5)
            copy_left(7)
            copy_turn(6)
            copy_left(8)
            relu1(0)
            relu1(2)
            act.wait_ge(layer2_done, 1)
            nc.scalar.activation(h2[:, 0, :], h2_ps[0][:, :], ACT.Relu, bias=b2_sb[:, 0:1]).then_inc(h2_ready[0], 1)
            act.wait_ge(layer3_done, 1)
            nc.scalar.activation(y[:, 0:BATCH // HALVES], y_ps[:, 0, :], ACT.Copy).then_inc(y_ready, 1)

        @block.tensor
        def _(pe):
            def quads(first, end, between=lambda u: keep_warm(2)):
                for u in range(first, end):
                    if u >= 2:
                        pe.wait_ge(onehots_ready, u - 1)
                    for f in range(2 * u, min(2 * u + 2, NS)):
                        last = nc.tensor.matmul(quad_banks(u)[:, f % 2, :], quad_w_sb[:, :],
                                                query[:, f * BATCH:(f + 1) * BATCH], start=True, stop=True)
                    last.then_inc(quads_ready, 1)
                    between(u)

            def half_sum(g, part=0, of=1):
                a, b = half_blocks(g)
                products = DIM // HALF_WIDTH
                if part == 0:
                    pe.wait_ge(tables_loaded[g][HALF_SUMMED[g][0] >= GROUPS[g][1] // 2], 16)
                    if g == 3:
                        pe.wait_ge(rows_summed, 1)
                for k in range(part * products // of, (part + 1) * products // of):
                    last = nc.tensor.matmul(half_ps(g), ident_f,
                                            tables_sb[:, a:b, k * HALF_WIDTH:(k + 1) * HALF_WIDTH],
                                            start=(k == 0), stop=(k == products - 1))
                if part == of - 1:
                    last.then_inc(half_summed, 1)

            def keep_warm(n, bank=turn_ps):
                for _ in range(n):
                    nc.tensor.matmul(bank[:, :], zeros[:, 0:P], zeros[:, :], start=True, stop=True)

            def lookups(g):
                first, count, blocks = GROUPS[g]
                n = SPLIT * blocks
                pe.wait_ge(row_parts_ready, g + 1)
                pe.wait_ge(onehots_ready, (first + count + 1) // 2)
                if g >= 1:
                    pe.wait_ge(lookups_masked, g)
                for t in range(TILES):
                    for f in range(count):
                        at = (t * count + f) * n
                        src = SPLIT * FIRST_BLOCK[g] + f * n
                        last = nc.tensor.matmul(look_ps[:, at:at + n], onehot[:, first + f, t * P:(t + 1) * P],
                                                row_parts[:, src:src + n], start=True, stop=True)
                last.then_inc(lookups_ready, 1)

            def turn(n):
                c0, c1, t0, t1 = TURNS[n]
                for t in range(t0, t1):
                    last = nc.tensor.transpose(turn_bf[c0:c1, t * P:(t + 1) * P], parts[:, t, c0:c1], ident)
                last.then_inc(turned, 1)

            def select(n):
                chunks, t0, t1 = STEPS[n]
                w = (t1 - t0) * P
                rows = {0: 64, 2: 96}.get(n, P)
                if n >= 1:
                    pe.wait_ge(z_ready, n)
                for side in range(2):
                    for i, c in enumerate(chunks):
                        last = nc.tensor.matmul(pair_ps[:, side, i * w:(i + 1) * w], sel_sb[0:rows, SELECTOR[c] + side, :],
                                                parts_t[0:rows, t0 * P:t1 * P], start=True, stop=True)
                last.then_inc(pairs_selected, 1)

            def layer1(n, between=lambda i: None):
                chunks, t0, t1 = STEPS[n]
                last_step = n == len(STEPS) - 1
                pe.wait_ge(z_ready, n + 1)
                for c in chunks:
                    pe.wait_ge(w1_loaded[c], 16)
                order = [(c, m) for c in chunks for m in range(HIDDEN1 // P)]
                if last_step:
                    order.sort(key=lambda cm: cm[1])
                for i, (c, m) in enumerate(order):
                    rows = CHUNK_ROWS[c]
                    last = nc.tensor.matmul(h1_ps[:, m, t0 * P:t1 * P], w1_sb[0:rows, c, m * P:(m + 1) * P],
                                            z[0:rows, c, t0 * P:t1 * P], start=(n == 0), stop=(c == CHUNKS - 1),
                                            skip_group_check=True)
                    if last_step and c == CHUNKS - 1:
                        last.then_inc(layer1_done, 1)
                    between(i)

            def layer2():
                for k in range(HIDDEN1 // P):
                    pe.wait_ge(h1_ready[k], 1)
                    for m in range(HIDDEN2 // P):
                        last = nc.tensor.matmul(h2_ps[m][:, :], w2_sb[:, k, m * P:(m + 1) * P], h1[:, k, :],
                                                start=(k == 0), stop=(k == HIDDEN1 // P - 1))
                        if k == HIDDEN1 // P - 1:
                            last.then_inc(layer2_done, 1)

            def layer3():
                width = BATCH // HALVES
                for k in range(HIDDEN2 // P):
                    pe.wait_ge(h2_ready[k], 1)
                    for half in range(HALVES):
                        last = nc.tensor.matmul(y_ps[:, half, :], w3_sb[:, k:k + 1],
                                                h2[:, k, half * width:(half + 1) * width],
                                                start=(k == 0), stop=(k == HIDDEN2 // P - 1))
                        if k == HIDDEN2 // P - 1:
                            last.then_inc(layer3_done, 1)

            pe.wait_ge(warmup_ready, 1)
            keep_warm(20)
            pe.wait_ge(quad_w_loaded, 16)
            pe.wait_ge(query_loaded, 3 * 16)
            quads(0, 4)
            lookups(0)
            quads(4, 6, lambda u: half_sum(1, u - 4, 2))
            quads(6, 8)
            lookups(1)
            quads(8, 10, lambda u: half_sum(2, u - 8, 2))
            quads(10, 12, lambda u: half_sum(3, u - 10, 4))
            lookups(2)
            quads(12, 14, lambda u: half_sum(3, u - 10, 4))
            pe.wait_ge(sel_loaded[0], 16)
            pe.wait_ge(small_parts_ready, 3)
            turn(0)
            quads(14, QUADS, lambda u: None)
            pe.wait_ge(rows_summed, 3)
            pe.wait_ge(parts_t_ready, 1)
            select(0)
            lookups(3)
            pe.wait_ge(onehots_ready, QUADS)
            half_sum(4)
            pe.wait_ge(dense_loaded, 16)

            def pairs_of_early_tiles(i):
                if i == 1:
                    pe.wait_ge(large_parts_ready, 2)
                    turn(1)
                if i == 2:
                    pe.wait_ge(parts_t_ready, 2)
                    select(1)
                    pe.wait_ge(rows_summed, 4)

            layer1(0, pairs_of_early_tiles)
            lookups(4)
            layer1(1, lambda i: i == 2 and (pe.wait_ge(small_parts_ready, 5), turn(2)))
            pe.wait_ge(parts_t_ready, 3)
            pe.wait_ge(sel_loaded[1], 16)
            select(2)
            keep_warm(4)
            select(3)
            layer1(2, lambda i: (i == 1 and lookups(5), i == 3 and select(4)))
            layer1(3, lambda i: i == 2 and (pe.wait_ge(large_parts_ready, 3), turn(3)))
            pe.wait_ge(parts_t_ready, 4)
            select(5)
            layer1(4, lambda i: (i == 1 and (pe.wait_ge(small_parts_ready, 6), turn(4)), i == 3 and lookups(6)))
            pe.wait_ge(parts_t_ready, 5)
            select(6)
            layer1(5, lambda i: i == 4 and (pe.wait_ge(small_parts_ready, 7), turn(5)))
            pe.wait_ge(parts_t_ready, 6)
            select(7)
            layer1(6, lambda i: i == 1 and (pe.wait_ge(large_parts_ready, 4), turn(6)))
            pe.wait_ge(parts_t_ready, 7)
            select(8)
            layer1(7)
            layer1(8)
            pe.wait_ge(w2_loaded, 16)
            layer2()
            layer3()

        @block.vector
        def _(dve):
            chain = [0]

            def link(instruction):
                chain[0] += 1
                instruction.then_inc(dve_steps, 1)
                dve.wait_ge(dve_steps, chain[0])

            def split(total, rest, hi, mid, lo, done, between=(lambda: None, lambda: None)):
                nc.vector.tensor_copy(hi, total).then_inc(dve_steps, 1)
                chain[0] += 1
                after_hi = chain[0]
                between[0]()
                dve.wait_ge(dve_steps, after_hi)
                nc.vector.tensor_tensor(rest, total, hi, ALU.subtract).then_inc(dve_steps, 1)
                chain[0] += 1
                after_rest = chain[0]
                between[1]()
                dve.wait_ge(dve_steps, after_rest)
                link(nc.vector.tensor_copy(mid, rest))
                nc.vector.tensor_tensor(lo, rest, mid, ALU.subtract).then_inc(done, 1)

            def sum_rows(g, half):
                _, count, blocks = GROUPS[g]
                mine = [f for f in ((range(count // 2), range(count // 2, count))[half])
                        if f not in ACT_SUMMED.get(g, []) and f not in range(*HALF_SUMMED.get(g, (0, 0)))]
                first, end = FIRST_BLOCK[g] + mine[0] * blocks, FIRST_BLOCK[g] + (mine[-1] + 1) * blocks
                dve.wait_ge(tables_loaded[g][half], 16)
                nc.vector.tensor_reduce(row_sums[:, first:end], tables_sb[:, first:end, :], op=ALU.add, axis=AX.X)\
                  .then_inc(dve_steps, 1)
                chain[0] += 1

            def sum_halves(g):
                a, b = half_blocks(g)
                dve.wait_ge(half_summed, g)
                nc.vector.tensor_reduce(row_sums[:, a:b], half_ps(g), op=ALU.add, axis=AX.X)\
                  .then_inc(rows_summed, 1)
                dve.wait_ge(rows_summed, g)

            def split_rows(g, between=(lambda: None, lambda: None)):
                _, count, blocks = GROUPS[g]
                a, b = FIRST_BLOCK[g], FIRST_BLOCK[g + 1]
                dve.wait_ge(dve_steps, chain[0])
                if g in ACT_SUMMED:
                    dve.wait_ge(rows_summed_act, sum(len(fs) for h, fs in ACT_SUMMED.items() if h <= g))
                by_part = row_parts[:, SPLIT * a:SPLIT * b].rearrange("p (f s c) -> p f s c", s=SPLIT, c=blocks)
                split(row_sums[:, a:b].rearrange("p (f c) -> p f c", c=blocks),
                      row_rest[:, a:b].rearrange("p (f c) -> p f c", c=blocks),
                      by_part[:, :, 0, :], by_part[:, :, 1, :], by_part[:, :, 2, :], row_parts_ready, between)

            def keep_block(g):
                _, count, blocks = GROUPS[g]
                n = TILES * count
                keep = mask[:, TILES * FIRST_BLOCK[g]:TILES * FIRST_BLOCK[g + 1]].rearrange("p (n c) -> p n c", c=blocks)
                dve.wait_ge(lookups_ready, g + 1)
                nc.vector.tensor_tensor(
                    masked[:, g % 2, 0:n * SPLIT * blocks].rearrange("p (n s c) -> p n s c", s=SPLIT, c=blocks),
                    look_ps[:, 0:n * SPLIT * blocks].rearrange("p (n s c) -> p n s c", s=SPLIT, c=blocks),
                    keep.unsqueeze(2).to_broadcast([P, n, SPLIT, blocks]), ALU.mult).then_inc(lookups_masked, 1)

            def sum_blocks(g):
                first, count, blocks = GROUPS[g]
                place = PLACE[SMALL[first]]
                dve.wait_ge(lookups_masked, g + 1)
                if g in (3, 5, 6):
                    dve.wait_ge(turned, {3: 1, 5: 3, 6: 5}[g])
                with nc.allow_low_precision(reason="a sum of one bfloat16 value and zeros is exact"):
                    nc.vector.tensor_reduce(
                        parts[:, :, place:place + SPLIT * count],
                        masked[:, g % 2, 0:TILES * count * SPLIT * blocks]
                        .rearrange("p (t m c) -> p t m c", t=TILES, c=blocks),
                        op=ALU.add, axis=AX.X).then_inc(small_parts_ready, 1)

            def large_parts(t):
                dve.wait_ge(rows_gathered[t], NL * 16)
                link(nc.vector.tensor_reduce(large_sums[:, t, :], gathered[:, t, :, :], op=ALU.add, axis=AX.X))
                by_part = parts[:, t, 3 * SET:3 * SET + SPLIT * NL].rearrange("p (f s) -> p f s", s=SPLIT)
                split(large_sums[:, t, :], large_rest[:, t, :], by_part[:, :, 0], by_part[:, :, 1], by_part[:, :, 2],
                      large_parts_ready)

            def multiply_pairs(n):
                chunks, t0, t1 = STEPS[n]
                w = (t1 - t0) * P
                rows = min(CHUNK_PAIRS[c] for c in chunks) if len(chunks) == 1 else P
                cols = slice(0, len(chunks) * w)
                dve.wait_ge(left_copied, n + 1)
                nc.vector.tensor_tensor(
                    z[0:rows, chunks[0]:chunks[0] + len(chunks), t0 * P:t1 * P],
                    pair_ps[0:rows, 1, cols].rearrange("p (c w) -> p c w", w=w),
                    left[0:rows, n % 2, cols].rearrange("p (c w) -> p c w", w=w), ALU.mult).then_inc(z_ready, 1)

            def relu1(m):
                dve.wait_ge(layer1_done, m + 1)
                nc.vector.tensor_scalar(h1[:, m, :], h1_ps[:, m, :], 0.0, None, ALU.max).then_inc(h1_ready[m], 1)

            dve.wait_ge(ids_loaded, 16)
            link(nc.vector.tensor_scalar(row_of[:, :], flat_ids, P - 1, None, ALU.bitwise_and))
            nc.vector.tensor_copy(digits[:, 2, :], row_of[:, :])
            link(nc.vector.tensor_tensor(row_sq[:, :], row_of[:, :], row_of[:, :], ALU.mult))
            nc.vector.tensor_scalar(row_sq_digit[:, 0, :], row_sq[:, :], 7, None, ALU.logical_shift_right)
            link(nc.vector.tensor_scalar(row_sq_digit[:, 1, :], row_sq[:, :], P - 1, None, ALU.bitwise_and))
            nc.vector.tensor_copy(digits[:, 0:2, :], row_sq_digit[:, :, :]).then_inc(digits_ready, 1)
            link(nc.vector.tensor_scalar(block_of[:, :], block_ids, 7, None, ALU.logical_shift_right))
            dve.wait_ge(consts_loaded, 16)
            for g0, g1 in ((0, 3), (3, len(GROUPS))):
                a, b, blocks = GROUPS[g0][0], GROUPS[g1 - 1][0] + GROUPS[g1 - 1][1], GROUPS[g0][2]
                n = TILES * (b - a)
                at = TILES * FIRST_BLOCK[g0]
                link(nc.vector.tensor_tensor(
                    mask[:, at:at + n * blocks].rearrange("p (n c) -> p n c", c=blocks),
                    block_of[:, TILES * a:TILES * b].unsqueeze(2).to_broadcast([P, n, blocks]),
                    block_iota[:, 0:blocks].unsqueeze(1).to_broadcast([P, n, blocks]), ALU.is_equal))
            dve.wait_ge(zeros_set, 2)
            sum_rows(0, 0)
            sum_rows(0, 1)
            split_rows(0)
            sum_rows(1, 0)
            sum_rows(1, 1)
            keep_block(0)
            sum_blocks(0)
            sum_rows(2, 0)
            sum_halves(1)
            split_rows(1)
            sum_rows(2, 1)
            keep_block(1)
            sum_blocks(1)
            sum_rows(3, 0)
            sum_halves(2)
            split_rows(2)
            large_parts(0)
            keep_block(2)
            sum_blocks(2)
            sum_halves(3)
            split_rows(3)
            sum_rows(4, 0)
            keep_block(3)
            multiply_pairs(0)
            sum_blocks(3)
            large_parts(1)
            sum_halves(4)
            sum_rows(4, 1)
            split_rows(4)
            multiply_pairs(1)
            keep_block(4)
            sum_blocks(4)
            sum_rows(5, 1)
            split_rows(5)
            multiply_pairs(2)
            large_parts(2)
            multiply_pairs(3)
            keep_block(5)
            sum_blocks(5)
            multiply_pairs(4)
            sum_rows(6, 1)
            multiply_pairs(5)
            split_rows(6)
            keep_block(6)
            sum_blocks(6)
            multiply_pairs(6)
            large_parts(3)
            multiply_pairs(7)
            multiply_pairs(8)
            relu1(1)
            relu1(3)
            dve.wait_ge(layer2_done, 2)
            nc.vector.tensor_scalar(h2[:, 1, :], h2_ps[1][:, :], b2_sb[:, 1:2], 0.0, ALU.add, ALU.max)\
              .then_inc(h2_ready[1], 1)
            dve.wait_ge(layer3_done, 2)
            nc.vector.tensor_copy(y[:, BATCH // HALVES:], y_ps[:, 1, :]).then_inc(y_ready, 1)


def kernel(**inputs):
    import ml_dtypes
    import concourse.bacc as bacc
    from concourse.bass_utils import run_bass_kernel_spmd

    a = {k: np.asarray(v) for k, v in inputs.items()}
    for f in range(NUM_FIELDS):
        assert -(-a[f"tbl_{f}"].shape[0] // P) == BLOCKS[f]

    ids = a["ids"]
    by_tile = ids.reshape(TILES, P, NUM_FIELDS).transpose(1, 0, 2)
    ids_all = np.concatenate(
        [by_tile[:, :, LARGE].reshape(P, -1)]
        + [by_tile[:, :, SMALL[s:s + n]].reshape(P, -1) for s, n, _ in GROUPS]
        + [np.ascontiguousarray(ids[:, SMALL].T).reshape(P, -1)], axis=1)

    def blocked(f):
        rows = a[f"tbl_{f}"]
        padded = np.zeros((BLOCKS[f] * P, DIM), rows.dtype)
        padded[:rows.shape[0]] = rows
        return padded.reshape(BLOCKS[f], P, DIM).transpose(1, 0, 2)

    tables = np.concatenate([blocked(f) for f in SMALL], axis=1)

    chunks = chunks_of_pairs()
    number = {}
    for i in range(NUM_FIELDS):
        for j in range(i + 1, NUM_FIELDS):
            number[i, j] = len(number)
    w1 = np.zeros((P, CHUNKS, HIDDEN1), np.float32)
    selectors = np.zeros((P, 2 * CHUNKS + 1, P), ml_dtypes.bfloat16)
    for c, pairs in enumerate(chunks):
        w1[:len(pairs), c] = a["W_top1"][[number[p] for p in pairs]]
        for r, pair in enumerate(pairs):
            for side in range(2):
                selectors[PLACE[pair[side]]:PLACE[pair[side]] + SPLIT, SELECTOR[c] + side, r] = 1
    selectors[:, 0] = np.eye(P)
    w1[CHUNK_PAIRS[0]:CHUNK_ROWS[0] - 1, 0] = a["W_top1"][len(number):]
    w1[CHUNK_ROWS[0] - 1, 0] = a["b_top1"]
    dense_t = np.concatenate([a["dense_ctx"].T, np.ones((1, BATCH), np.float32)])
    w2 = a["W_top2"].reshape(HIDDEN1 // P, P, HIDDEN2).transpose(1, 0, 2)

    q = np.arange(P)
    consts = np.concatenate([(1 - q * q)[:, None], np.tile(np.arange(WIDE), (P, 1)),
                             a["b_top2"].reshape(-1, P).T, a["W_top3"].reshape(-1, P).T, np.eye(P)],
                            axis=1).astype(np.float32)
    quad_w = np.stack([np.full(P, -128), np.full(P, -1), 2 * q]).astype(ml_dtypes.bfloat16)

    arrays = {"ids": ids_all, "tables": tables}
    arrays.update({f"large_{f}": a[f"tbl_{f}"] for f in LARGE})
    arrays.update(consts=consts, selectors=selectors, quad_w=quad_w, w1=w1, w2=w2, dense_t=dense_t)
    arrays = {k: np.ascontiguousarray(v) for k, v in arrays.items()}

    nc = bacc.Bacc("TRN2", target_bir_lowering=False, num_devices=1)
    ap = {k: nc.dram_tensor(k, v.shape, mybir.dt.from_np(v.dtype), kind="ExternalInput").ap()
          for k, v in arrays.items()}
    out = nc.dram_tensor("out", (BATCH, 1), mybir.dt.float32, kind="ExternalOutput").ap()
    build(nc, ap["ids"], ap["tables"], [ap[f"large_{f}"] for f in LARGE], ap["consts"], ap["selectors"],
          ap["quad_w"], ap["w1"], ap["w2"], ap["dense_t"], out)
    result = run_bass_kernel_spmd(nc, [arrays], core_ids=[0])
    return result.results[0]["out"]
```
